# Optimizing a Trainium2 kernel written in Bass

```python
import numpy as np
import jax
import jax.numpy as jnp

def _softmax(x, axis=-1):
    return jax.nn.softmax(x, axis=axis)

def _gelu(x):
    return jax.nn.gelu(x, approximate=True)

def _silu(x):
    return jax.nn.silu(x)

def _sigmoid(x):
    return jax.nn.sigmoid(x)

def _layernorm(x, axis=-1, eps=1e-05):
    m = jnp.mean(x, axis=axis, keepdims=True)
    v = jnp.var(x, axis=axis, keepdims=True)
    return (x - m) / jnp.sqrt(v + eps)

def _scatter_add(tgt, idx, src, axis=0):
    return tgt.at[idx].add(src)

def _segment_sum(src, seg, n):
    return jax.ops.segment_sum(src, seg, n)
kernel_name = 'mk_dlrm_tower_d1_rec_r8_9814b5'

def setup_inputs(seed: int=0):
    np.random.seed(seed)
    _w = jnp.asarray

    def _rec_inputs():
        import jax
        import jax.numpy as jnp
        _tk = jax.random.key(seed)
        dense_ctx = jax.random.normal(jax.random.fold_in(_tk, 190), (2048, 16), jnp.float32)
        ids = jnp.stack([jax.random.randint(jax.random.fold_in(_tk, 200 + f), (2048,), 0, v, jnp.int32) for f, v in enumerate([12500, 1250, 1000, 12500, 125000, 125000, 1000, 125000, 1250, 1000, 12500, 1250, 125000, 12500, 1250, 1000, 12500, 12500, 125000, 12500, 125000, 1000, 1000, 1000, 12500, 12500, 12500, 1250, 1000, 1000, 1000, 12500, 1000, 1250, 12500, 1000, 1000, 1250, 1000, 12500])], axis=1)
        tbl_0 = 0.05 * jax.random.normal(jax.random.fold_in(_tk, 500 + 0), (12500, 32), jnp.float32)
        tbl_1 = 0.05 * jax.random.normal(jax.random.fold_in(_tk, 500 + 1), (1250, 32), jnp.float32)
        tbl_2 = 0.05 * jax.random.normal(jax.random.fold_in(_tk, 500 + 2), (1000, 32), jnp.float32)
        tbl_3 = 0.05 * jax.random.normal(jax.random.fold_in(_tk, 500 + 3), (12500, 32), jnp.float32)
        tbl_4 = 0.05 * jax.random.normal(jax.random.fold_in(_tk, 500 + 4), (125000, 32), jnp.float32)
        tbl_5 = 0.05 * jax.random.normal(jax.random.fold_in(_tk, 500 + 5), (125000, 32), jnp.float32)
        tbl_6 = 0.05 * jax.random.normal(jax.random.fold_in(_tk, 500 + 6), (1000, 32), jnp.float32)
        tbl_7 = 0.05 * jax.random.normal(jax.random.fold_in(_tk, 500 + 7), (125000, 32), jnp.float32)
        tbl_8 = 0.05 * jax.random.normal(jax.random.fold_in(_tk, 500 + 8), (1250, 32), jnp.float32)
        tbl_9 = 0.05 * jax.random.normal(jax.random.fold_in(_tk, 500 + 9), (1000, 32), jnp.float32)
        tbl_10 = 0.05 * jax.random.normal(jax.random.fold_in(_tk, 500 + 10), (12500, 32), jnp.float32)
        tbl_11 = 0.05 * jax.random.normal(jax.random.fold_in(_tk, 500 + 11), (1250, 32), jnp.float32)
        tbl_12 = 0.05 * jax.random.normal(jax.random.fold_in(_tk, 500 + 12), (125000, 32), jnp.float32)
        tbl_13 = 0.05 * jax.random.normal(jax.random.fold_in(_tk, 500 + 13), (12500, 32), jnp.float32)
        tbl_14 = 0.05 * jax.random.normal(jax.random.fold_in(_tk, 500 + 14), (1250, 32), jnp.float32)
        tbl_15 = 0.05 * jax.random.normal(jax.random.fold_in(_tk, 500 + 15), (1000, 32), jnp.float32)
        tbl_16 = 0.05 * jax.random.normal(jax.random.fold_in(_tk, 500 + 16), (12500, 32), jnp.float32)
        tbl_17 = 0.05 * jax.random.normal(jax.random.fold_in(_tk, 500 + 17), (12500, 32), jnp.float32)
        tbl_18 = 0.05 * jax.random.normal(jax.random.fold_in(_tk, 500 + 18), (125000, 32), jnp.float32)
        tbl_19 = 0.05 * jax.random.normal(jax.random.fold_in(_tk, 500 + 19), (12500, 32), jnp.float32)
        tbl_20 = 0.05 * jax.random.normal(jax.random.fold_in(_tk, 500 + 20), (125000, 32), jnp.float32)
        tbl_21 = 0.05 * jax.random.normal(jax.random.fold_in(_tk, 500 + 21), (1000, 32), jnp.float32)
        tbl_22 = 0.05 * jax.random.normal(jax.random.fold_in(_tk, 500 + 22), (1000, 32), jnp.float32)
        tbl_23 = 0.05 * jax.random.normal(jax.random.fold_in(_tk, 500 + 23), (1000, 32), jnp.float32)
        tbl_24 = 0.05 * jax.random.normal(jax.random.fold_in(_tk, 500 + 24), (12500, 32), jnp.float32)
        tbl_25 = 0.05 * jax.random.normal(jax.random.fold_in(_tk, 500 + 25), (12500, 32), jnp.float32)
        tbl_26 = 0.05 * jax.random.normal(jax.random.fold_in(_tk, 500 + 26), (12500, 32), jnp.float32)
        tbl_27 = 0.05 * jax.random.normal(jax.random.fold_in(_tk, 500 + 27), (1250, 32), jnp.float32)
        tbl_28 = 0.05 * jax.random.normal(jax.random.fold_in(_tk, 500 + 28), (1000, 32), jnp.float32)
        tbl_29 = 0.05 * jax.random.normal(jax.random.fold_in(_tk, 500 + 29), (1000, 32), jnp.float32)
        tbl_30 = 0.05 * jax.random.normal(jax.random.fold_in(_tk, 500 + 30), (1000, 32), jnp.float32)
        tbl_31 = 0.05 * jax.random.normal(jax.random.fold_in(_tk, 500 + 31), (12500, 32), jnp.float32)
        tbl_32 = 0.05 * jax.random.normal(jax.random.fold_in(_tk, 500 + 32), (1000, 32), jnp.float32)
        tbl_33 = 0.05 * jax.random.normal(jax.random.fold_in(_tk, 500 + 33), (1250, 32), jnp.float32)
        tbl_34 = 0.05 * jax.random.normal(jax.random.fold_in(_tk, 500 + 34), (12500, 32), jnp.float32)
        tbl_35 = 0.05 * jax.random.normal(jax.random.fold_in(_tk, 500 + 35), (1000, 32), jnp.float32)
        tbl_36 = 0.05 * jax.random.normal(jax.random.fold_in(_tk, 500 + 36), (1000, 32), jnp.float32)
        tbl_37 = 0.05 * jax.random.normal(jax.random.fold_in(_tk, 500 + 37), (1250, 32), jnp.float32)
        tbl_38 = 0.05 * jax.random.normal(jax.random.fold_in(_tk, 500 + 38), (1000, 32), jnp.float32)
        tbl_39 = 0.05 * jax.random.normal(jax.random.fold_in(_tk, 500 + 39), (12500, 32), jnp.float32)
        _rk = jax.random.fold_in(_tk, 7)
        W_top1 = 0.0354441 * jax.random.normal(jax.random.fold_in(_tk, 801), (796, 512), jnp.float32)
        W_top2 = 0.0441942 * jax.random.normal(jax.random.fold_in(_tk, 802), (512, 256), jnp.float32)
        W_top3 = 0.0625 * jax.random.normal(jax.random.fold_in(_tk, 803), (256, 1), jnp.float32)
        b_top1 = jnp.zeros((512,), jnp.float32)
        b_top2 = jnp.zeros((256,), jnp.float32)
        return (dense_ctx, ids, tbl_0, tbl_1, tbl_2, tbl_3, tbl_4, tbl_5, tbl_6, tbl_7, tbl_8, tbl_9, tbl_10, tbl_11, tbl_12, tbl_13, tbl_14, tbl_15, tbl_16, tbl_17, tbl_18, tbl_19, tbl_20, tbl_21, tbl_22, tbl_23, tbl_24, tbl_25, tbl_26, tbl_27, tbl_28, tbl_29, tbl_30, tbl_31, tbl_32, tbl_33, tbl_34, tbl_35, tbl_36, tbl_37, tbl_38, tbl_39, W_top1, b_top1, W_top2, b_top2, W_top3)
    dense_ctx, ids, tbl_0, tbl_1, tbl_2, tbl_3, tbl_4, tbl_5, tbl_6, tbl_7, tbl_8, tbl_9, tbl_10, tbl_11, tbl_12, tbl_13, tbl_14, tbl_15, tbl_16, tbl_17, tbl_18, tbl_19, tbl_20, tbl_21, tbl_22, tbl_23, tbl_24, tbl_25, tbl_26, tbl_27, tbl_28, tbl_29, tbl_30, tbl_31, tbl_32, tbl_33, tbl_34, tbl_35, tbl_36, tbl_37, tbl_38, tbl_39, W_top1, b_top1, W_top2, b_top2, W_top3 = _rec_inputs()

    def _L0_rec_setup():
        import jax, jax.numpy as jnp
        import numpy as np
        NUM_FIELDS = 40
        _I_IDX, _J_IDX = np.triu_indices(NUM_FIELDS, k=1)
        key = jax.random.key(seed)
        k1, k2 = jax.random.split(key)
        batch, num_fields, embed_dim = (1024, NUM_FIELDS, 32)
        num_interactions = num_fields * (num_fields - 1) // 2
        embeddings = jax.random.normal(k1, (batch, num_fields, embed_dim), dtype=jnp.float32)
        W = jax.random.normal(k2, (num_interactions, embed_dim, embed_dim), dtype=jnp.float32)
        return {'embeddings': embeddings, 'W': W}
    _L0_rec_all = _L0_rec_setup()
    _L0_rec_in = {k: v for k, v in _L0_rec_all.items() if k in ('W',)}
    del _L0_rec_all
    return {'dense_ctx': dense_ctx, 'ids': ids, 'tbl_0': tbl_0, 'tbl_1': tbl_1, 'tbl_2': tbl_2, 'tbl_3': tbl_3, 'tbl_4': tbl_4, 'tbl_5': tbl_5, 'tbl_6': tbl_6, 'tbl_7': tbl_7, 'tbl_8': tbl_8, 'tbl_9': tbl_9, 'tbl_10': tbl_10, 'tbl_11': tbl_11, 'tbl_12': tbl_12, 'tbl_13': tbl_13, 'tbl_14': tbl_14, 'tbl_15': tbl_15, 'tbl_16': tbl_16, 'tbl_17': tbl_17, 'tbl_18': tbl_18, 'tbl_19': tbl_19, 'tbl_20': tbl_20, 'tbl_21': tbl_21, 'tbl_22': tbl_22, 'tbl_23': tbl_23, 'tbl_24': tbl_24, 'tbl_25': tbl_25, 'tbl_26': tbl_26, 'tbl_27': tbl_27, 'tbl_28': tbl_28, 'tbl_29': tbl_29, 'tbl_30': tbl_30, 'tbl_31': tbl_31, 'tbl_32': tbl_32, 'tbl_33': tbl_33, 'tbl_34': tbl_34, 'tbl_35': tbl_35, 'tbl_36': tbl_36, 'tbl_37': tbl_37, 'tbl_38': tbl_38, 'tbl_39': tbl_39, 'W_top1': W_top1, 'b_top1': b_top1, 'W_top2': W_top2, 'b_top2': b_top2, 'W_top3': W_top3, 'L0_rec_W': _L0_rec_in['W']}

def reference(dense_ctx, ids, tbl_0, tbl_1, tbl_2, tbl_3, tbl_4, tbl_5, tbl_6, tbl_7, tbl_8, tbl_9, tbl_10, tbl_11, tbl_12, tbl_13, tbl_14, tbl_15, tbl_16, tbl_17, tbl_18, tbl_19, tbl_20, tbl_21, tbl_22, tbl_23, tbl_24, tbl_25, tbl_26, tbl_27, tbl_28, tbl_29, tbl_30, tbl_31, tbl_32, tbl_33, tbl_34, tbl_35, tbl_36, tbl_37, tbl_38, tbl_39, W_top1, b_top1, W_top2, b_top2, W_top3, L0_rec_W):
    import jax
    import jax.numpy as jnp

    def _L0_rec_ref(embeddings, W):
        import jax, jax.numpy as jnp
        import numpy as np
        NUM_FIELDS = 40
        _I_IDX, _J_IDX = np.triu_indices(NUM_FIELDS, k=1)
        vi = embeddings[:, _I_IDX, :]
        vj = embeddings[:, _J_IDX, :]
        return jnp.einsum('bke,kef,bkf->bk', vi, W, vj)
    e = jnp.stack([tbl_0[ids[:, 0]], tbl_1[ids[:, 1]], tbl_2[ids[:, 2]], tbl_3[ids[:, 3]], tbl_4[ids[:, 4]], tbl_5[ids[:, 5]], tbl_6[ids[:, 6]], tbl_7[ids[:, 7]], tbl_8[ids[:, 8]], tbl_9[ids[:, 9]], tbl_10[ids[:, 10]], tbl_11[ids[:, 11]], tbl_12[ids[:, 12]], tbl_13[ids[:, 13]], tbl_14[ids[:, 14]], tbl_15[ids[:, 15]], tbl_16[ids[:, 16]], tbl_17[ids[:, 17]], tbl_18[ids[:, 18]], tbl_19[ids[:, 19]], tbl_20[ids[:, 20]], tbl_21[ids[:, 21]], tbl_22[ids[:, 22]], tbl_23[ids[:, 23]], tbl_24[ids[:, 24]], tbl_25[ids[:, 25]], tbl_26[ids[:, 26]], tbl_27[ids[:, 27]], tbl_28[ids[:, 28]], tbl_29[ids[:, 29]], tbl_30[ids[:, 30]], tbl_31[ids[:, 31]], tbl_32[ids[:, 32]], tbl_33[ids[:, 33]], tbl_34[ids[:, 34]], tbl_35[ids[:, 35]], tbl_36[ids[:, 36]], tbl_37[ids[:, 37]], tbl_38[ids[:, 38]], tbl_39[ids[:, 39]]], axis=1)
    z = _L0_rec_ref(e, L0_rec_W)
    z = z.reshape(z.shape[0], -1)
    h = jnp.concatenate([z, dense_ctx], axis=1)
    h = jnp.maximum(h @ W_top1 + b_top1, 0.0)
    h = jnp.maximum(h @ W_top2 + b_top2, 0.0)
    y = h @ W_top3
    return y

_drawn_inputs = setup_inputs


def setup_inputs(seed=0):
    import zlib

    import numpy as np

    out = dict(_drawn_inputs(seed))
    spreads = {'b_top1': (0.0, 0.1), 'b_top2': (0.0, 0.1)}
    factors = {}
    for name, (base, spread) in spreads.items():
        noise = np.random.default_rng([zlib.crc32(name.encode()), seed]).standard_normal(out[name].shape)
        drawn = base * np.exp(spread * noise) if base else spread * noise
        out[name] = jnp.asarray(drawn.astype(out[name].dtype))
    for name, factor in factors.items():
        out[name] = (out[name] * factor).astype(out[name].dtype)
    return out
```

```python
from contextlib import ExitStack

import concourse.bass as bass
from concourse import mybir
from concourse.alu_op_type import AluOpType as ALU

F32 = mybir.dt.float32
BF16 = mybir.dt.bfloat16
I32 = mybir.dt.int32
ACT = mybir.ActivationFunctionType

P = 128
FIELDS = 40
DIM = 32
PER = P // DIM
GROUPS = FIELDS // PER
BATCH = 2048
CHUNK = 512
CHUNKS = BATCH // CHUNK
BT = CHUNK // P
DENSE = 16
UNITS = GROUPS * GROUPS
TILES = 2 * UNITS
BATCH_TILES = 4
REDUCTIONS = TILES // BATCH_TILES
PER_BLOCK = P // (BATCH_TILES * PER)
ZBLOCKS = -(-REDUCTIONS // PER_BLOCK)
ZLAST = 2 * BATCH_TILES * PER
H1, H2 = 512, 256
M1, M2 = H1 // P, H2 // P

GATHER_RING = 5
STACK_RING = 5
PRODUCT_RING = 4
PIECE_UNITS = 4
PIECES = UNITS // PIECE_UNITS
PCOLS = 2 * P * PIECE_UNITS

X_TILE = ((0, 0), (1, 0), (2, 0), (3, 2))
Y_TILE = ((0, 3), (1, 1), (2, 1), (3, 1))


STARTED = (range(4, 8), range(8, 10), range(10, 12), range(12, 14))
FIRST_PREPARED = (9, 17, 26, 38, 52, 68)
PREPARED = (5, 14, 24, 34, 45, 58)
AHEAD = (84, 87, 91, 96)


def unit_of(u):
    n = int(u ** 0.5)
    k = u - n * n
    g = GROUPS - 1 - n
    return n, g, GROUPS - 1 - k // 2, k % 2


def chunk_order(first, last):
    before = {u: [] for u in range(UNITS + 1)}

    def prepare(at, dc, n):
        for i, part in enumerate(("turn", "rest", "low")):
            before[at + i].append((part, dc, n))

    if first:
        for k in range(4):
            before[0].append(("piece", k))
        for n, at in enumerate((0, 0, 1, 4)):
            for part in ("turn", "rest", "low"):
                before[at].append((part, 0, n))
            before[at] += [("piece", k) for k in range(PIECES) if k in STARTED[n]]
        for n, at in enumerate(FIRST_PREPARED, 4):
            prepare(at, 0, n)
        for k in range(STARTED[3].stop, PIECES):
            before[9 + 4 * (k - STARTED[3].stop)].append(("piece", k))
    else:
        for n, at in enumerate(PREPARED, 4):
            prepare(at, 0, n)
    if not last:
        for n, at in enumerate(AHEAD):
            prepare(at, 1, n)
    order = []
    for u in range(UNITS):
        order += before[u]
        order.append(("unit", u))
        if u % 2 == 1 and u >= 3:
            order.append(("sum", (u - 3) // 2))
        if u % 16 == 3 and u > 16:
            order.append(("zout", (u - 3) // 16 - 1))
    order += before[UNITS]
    order.append(("sum", REDUCTIONS - 1))
    order.append(("zout", ZBLOCKS - 1))
    order.append(("mlp", 0))
    return order


def tower(nc, dense_t, ids, tables, w_pairs, w1, b1, w2, b2, w3, select, ident, out):
    with ExitStack() as ctx:
        def sb(name, shape, dt):
            return ctx.enter_context(nc.sbuf_tensor(name, shape, dt))

        def ps(name, shape):
            return ctx.enter_context(nc.psum_tensor(name, shape, F32))

        def sem(name):
            return ctx.enter_context(nc.semaphore(name))

        w_main = sb("w_main", [P, TILES * P], BF16)
        w_fine = sb("w_fine", [P, UNITS * P], BF16)
        stack_main = sb("stack_main", [P, STACK_RING, PER, CHUNK], BF16)
        stack_fine = sb("stack_fine", [P, STACK_RING, PER // 2, CHUNK], BF16)
        gathered = sb("gathered", [P, GATHER_RING, BT, P], F32)
        emb = sb("emb", [P, GROUPS, CHUNK], F32)
        parts = sb("parts", [P, 2, 3, CHUNK], BF16)
        rest = sb("rest", [P, CHUNK], F32)
        prod = sb("prod", [P, 2 * PRODUCT_RING, CHUNK], F32)
        z = sb("z", [P, ZBLOCKS, CHUNK], F32)
        w1_sb = sb("w1_sb", [P, ZBLOCKS, H1], F32)
        w2_sb = sb("w2_sb", [P, M1, H2], F32)
        w3_sb = sb("w3_sb", [P, M2], F32)
        b1_sb = sb("b1_sb", [P, M1], F32)
        b2_sb = sb("b2_sb", [P, M2], F32)
        sel = sb("sel", [P, PER_BLOCK, DIM], F32)
        ident_sb = sb("ident_sb", [P, P], F32)
        idx = sb("idx", [P, 2, BT, FIELDS // 2], I32)
        shared = sb("shared", [P, 3 * PCOLS], F32)
        w_raw = shared[:, 0:2 * PCOLS].rearrange("p (k n) -> p k n", k=2)
        w_rest = shared[:, 2 * PCOLS:3 * PCOLS]
        h1 = shared[:, 0:M1 * CHUNK].rearrange("p (m n) -> p m n", m=M1)
        h2 = shared[:, M1 * CHUNK:(M1 + M2) * CHUNK].rearrange("p (m n) -> p m n", m=M2)

        t_ps = ps("t_ps", [P, 4, CHUNK])
        turn_ps = ps("turn_ps", [P, 2, CHUNK])
        z_ps = ps("z_ps", [P, 2, CHUNK])

        parts_dram = nc.dram_tensor("parts_scratch", [2, 3, PER, DIM, CHUNK], BF16).ap()

        consts_loaded = sem("consts_loaded")
        idx_loaded = [sem(f"idx_loaded{i}") for i in range(2)]
        gather_done = [sem(f"gather_done{i}") for i in range(GATHER_RING)]
        turned = sem("turned")
        high_ready = sem("high_ready")
        rest_ready = sem("rest_ready")
        middle_ready = sem("middle_ready")
        low_ready = sem("low_ready")
        parts_stored = [sem(f"parts_stored{i}") for i in range(2)]
        stacked = [sem(f"stacked{i}") for i in range(STACK_RING)]
        t_ready = sem("t_ready")
        p_ready = sem("p_ready")
        summed = sem("summed")
        z_out = sem("z_out")
        dense_loaded = sem("dense_loaded")
        raw_loaded = [sem(f"raw_loaded{i}") for i in range(2)]
        w_high = sem("w_high")
        w_rest_ready = sem("w_rest_ready")
        w_middle = sem("w_middle")
        w_ready = sem("w_ready")
        h1_ready = sem("h1_ready")
        a1_ready = sem("a1_ready")
        h2_ready = sem("h2_ready")
        a2_ready = sem("a2_ready")
        y_ready = sem("y_ready")
        y_copied = sem("y_copied")
        y_stored = sem("y_stored")

        passed = [sem("passed_sp"), sem("passed_pool")]

        N_CONST = 7

        def wait(eng, s, value):
            if not (isinstance(value, int) and value <= 0):
                eng.wait_ge(s, value)

        def wait_alone(eng, s, value):
            wait(eng, s, value)
            if not isinstance(value, int):
                eng.sem_inc(passed[0] if eng is nc.sync else passed[1], 1)

        def chunks(eng, body):
            body(0, chunk_order(True, False))
            with eng.Fori(1, CHUNKS - 1) as c:
                body(c, chunk_order(False, False))
            body(CHUNKS - 1, chunk_order(False, True))

        block = ctx.enter_context(nc.Block())

        @block.sync
        def _(sp):
            def load_piece(k):
                wait_alone(sp, w_ready, k - 1)
                for r in range(PER):
                    sp.dma_start(w_raw[DIM * r:DIM * (r + 1), k % 2, :],
                                 w_pairs[:, PCOLS * k:PCOLS * (k + 1)]).then_inc(raw_loaded[k % 2], 16)

            def load_idx(c, half):
                lo = (1 - half) * (FIELDS // 2)
                sp.dma_start(idx[:, half], ids[c, :, :, lo:lo + FIELDS // 2]).then_inc(idx_loaded[half], 16)

            def stack(c, n):
                ring, par = n % STACK_RING, n % 2
                wait_alone(sp, low_ready, c * GROUPS + (n + 1))
                m = n - 2
                if m >= 0 or not isinstance(c, int) or c > 0:
                    cc, mm = (c, m) if m >= 0 else (c - 1, m + GROUPS)
                    wait_alone(sp, stacked[mm % STACK_RING], cc * 256 + 128 * (mm // STACK_RING + 1))
                sp.dma_start(parts_dram[par].rearrange("k q e b -> (q e) k b"),
                             parts[:, par]).then_inc(parts_stored[par], 16)
                wait_alone(sp, parts_stored[par], c * 80 + 16 * (n // 2 + 1))
                if n >= STACK_RING:
                    wait_alone(sp, t_ready, c * UNITS + (n - STACK_RING + 1) ** 2)
                else:
                    wait_alone(sp, t_ready, (c - 1) * UNITS + (n + STACK_RING + 1) ** 2)
                for s, k in enumerate((0, 1, 0, 1)):
                    sp.dma_start(stack_main[DIM * s:DIM * (s + 1), ring],
                                 parts_dram[par, k].rearrange("q e b -> e q b")).then_inc(stacked[ring], 16)
                for half in range(2):
                    src = parts_dram[par].rearrange("k (v h) e b -> k h e v b", h=2)
                    for s, k in enumerate((2, 0)):
                        row = 64 * half + DIM * s
                        sp.dma_start(stack_fine[row:row + DIM, ring], src[k, half]).then_inc(stacked[ring], 16)

            load_idx(0, 0)
            sp.dma_start(ident_sb[:, :], ident).then_inc(consts_loaded, 16)
            load_piece(0)
            load_piece(1)
            load_idx(0, 1)
            sp.dma_start(sel[:, :, :], select).then_inc(consts_loaded, 16)
            sp.dma_start(w1_sb[:, :, :], w1).then_inc(consts_loaded, 16)
            sp.dma_start(w2_sb[:, :, :], w2).then_inc(consts_loaded, 16)
            sp.dma_start(w3_sb[:, :], w3).then_inc(consts_loaded, 16)
            sp.dma_start(b1_sb[:, :], b1).then_inc(consts_loaded, 16)
            sp.dma_start(b2_sb[:, :], b2).then_inc(consts_loaded, 16)

            def body(c, order):
                for step, *a in order:
                    if step == "piece" and a[0] + 2 < PIECES:
                        load_piece(a[0] + 2)
                    if step == "low":
                        dc, n = a
                        stack(c + dc, n)
                        if dc == 1 and n == 0:
                            load_idx(c + 1, 1)
                        if dc == 0 and n == 5:
                            wait_alone(sp, h1_ready, c * M1)
                            sp.dma_start(z[ZLAST:ZLAST + DENSE, ZBLOCKS - 1, :],
                                         dense_t[c]).then_inc(dense_loaded, 16)
                            if order[-2] and ("turn", 1, 0) in order:
                                load_idx(c + 1, 0)
            chunks(sp, body)

        @block.gpsimd
        def _(pool):
            def gather(c, n):
                g, ring, half = GROUPS - 1 - n, n % GATHER_RING, n // GATHER_RING
                if n % GATHER_RING == 0:
                    wait_alone(pool, idx_loaded[half], c * 16 + 16)
                wait_alone(pool, turned, c * GROUPS + (n - GATHER_RING + 1))
                for t in range(BT):
                    for q in range(PER):
                        f = PER * g + q
                        col = f - (1 - half) * (FIELDS // 2)
                        nc.gpsimd.indirect_dma_start(
                            gathered[:, ring, t, DIM * q:DIM * (q + 1)], None, tables[f],
                            bass.IndirectOffsetOnAxis(ap=idx[:, half, t, col:col + 1], axis=0),
                        ).then_inc(gather_done[ring], 16)

            for n in range(GROUPS):
                gather(0, n)
            with pool.Fori(1, CHUNKS) as c:
                for n in range(GROUPS):
                    gather(c, n)

        @block.tensor
        def _(pe):
            def turn(c, n):
                ring = n % GATHER_RING
                uses = 2 if GROUPS == 2 * GATHER_RING else 1
                pe.wait_ge(gather_done[ring], c * (uses * 256) + 256 * (n // GATHER_RING + 1))
                wait(pe, high_ready, c * GROUPS + (n - 1))
                for t in range(BT):
                    last = nc.tensor.transpose(turn_ps[:, n % 2, P * t:P * (t + 1)],
                                               gathered[:, ring, t, :], ident_sb[:, :])
                last.then_inc(turned, 1)

            def main(out_ap, tile, cols, ring, q):
                nc.tensor.matmul(out_ap, w_main[:, P * tile + cols.start:P * tile + cols.stop],
                                 stack_main[:, ring, q, :], start=True, stop=False)

            def fine(out_ap, u, half, cols, ring, q):
                rows = slice(64 * half, 64 * half + 64)
                return nc.tensor.matmul(out_ap, w_fine[rows, P * u + cols.start:P * u + cols.stop],
                                        stack_fine[rows, ring, q // 2, :], start=False, stop=True)

            def unit(c, u, first):
                n, g, h, v = unit_of(u)
                ring, slot = n % STACK_RING, 2 * (u % 2)
                if u == n * n:
                    pe.wait_ge(stacked[ring], c * 256 + 128 * (n // STACK_RING + 1))
                if first and u % PIECE_UNITS == 0:
                    pe.wait_ge(w_ready, u // PIECE_UNITS + 1)
                if u >= 2:
                    wait(pe, p_ready, c * UNITS + (u - 1))
                elif u == 0:
                    wait(pe, a2_ready, c * M2)
                else:
                    wait(pe, y_copied, c)
                if h != g:
                    for half in range(2):
                        main(t_ps[:, slot + half, :], 2 * u + half, slice(0, P), ring, 2 * v + half)
                    for half in range(2):
                        last = fine(t_ps[:, slot + half, :], u, half, slice(0, P), ring, 2 * v + half)
                else:
                    for half, blocks in enumerate((X_TILE, Y_TILE)):
                        for p, q in blocks:
                            cols = slice(DIM * p, DIM * (p + 1))
                            main(t_ps[cols, slot + half, :], 2 * u + half, cols, ring, q)
                        for p, q in blocks:
                            cols = slice(DIM * p, DIM * (p + 1))
                            last = fine(t_ps[cols, slot + half, :], u, half, cols, ring, q)
                last.then_inc(t_ready, 1)

            def sum_pairs(c, b):
                k, r = b // PER_BLOCK, b % PER_BLOCK
                pe.wait_ge(p_ready, c * UNITS + (2 * b + 2))
                if r == 0 and k >= 2:
                    pe.wait_ge(z_out, c * ZBLOCKS + (k - 1))
                for j in range(BATCH_TILES):
                    at = (BATCH_TILES * b + j) % (2 * PRODUCT_RING)
                    if k < ZBLOCKS - 1:
                        rows, which, start, stop = slice(DIM * j, DIM * (j + 1)), r, r == 0, r == PER_BLOCK - 1
                    else:
                        which = BATCH_TILES * r + j
                        rows, start, stop = slice(0, DIM), which == 0, which == PER_BLOCK - 1
                    last = nc.tensor.matmul(z_ps[rows, k % 2, :], sel[:, which, :], prod[:, at, :],
                                            start=start, stop=stop)
                last.then_inc(summed, 1)

            def mlp(c):
                pe.wait_ge(p_ready, c * UNITS + UNITS)
                for k in range(ZBLOCKS):
                    rows = P
                    if k == ZBLOCKS - 2:
                        pe.wait_ge(z_out, c * ZBLOCKS + (ZBLOCKS - 1))
                    elif k == ZBLOCKS - 1:
                        rows = ZLAST + DENSE
                        pe.wait_ge(z_out, c * ZBLOCKS + ZBLOCKS)
                        pe.wait_ge(dense_loaded, c * 16 + 16)
                    elif k == 0:
                        pe.wait_ge(z_out, c * ZBLOCKS + (ZBLOCKS - 2))
                    for m in range(M1):
                        last = nc.tensor.matmul(t_ps[:, m, :], w1_sb[0:rows, k, P * m:P * (m + 1)],
                                                z[0:rows, k, :], start=(k == 0), stop=(k == ZBLOCKS - 1))
                        if k == ZBLOCKS - 1:
                            last.then_inc(h1_ready, 1)
                pe.wait_ge(a1_ready, c * M1 + M1)
                for m in range(M2):
                    for k in range(M1):
                        last = nc.tensor.matmul(t_ps[:, m, :], w2_sb[:, k, P * m:P * (m + 1)], h1[:, k, :],
                                                start=(k == 0), stop=(k == M1 - 1))
                    last.then_inc(h2_ready, 1)
                pe.wait_ge(a2_ready, c * M2 + M2)
                for k in range(M2):
                    last = nc.tensor.matmul(t_ps[0:1, 2, :], w3_sb[:, k:k + 1], h2[:, k, :],
                                            start=(k == 0), stop=(k == M2 - 1))
                last.then_inc(y_ready, 1)

            pe.wait_ge(consts_loaded, 16 * N_CONST)

            def body(c, order):
                for step, *a in order:
                    if step == "turn":
                        turn(c + a[0], a[1])
                    elif step == "unit":
                        unit(c, a[0], isinstance(c, int) and c == 0)
                    elif step == "sum":
                        sum_pairs(c, a[0])
                    elif step == "mlp":
                        mlp(c)
            chunks(pe, body)

        @block.scalar
        def _(act):
            def high(c, n):
                g = GROUPS - 1 - n
                act.wait_ge(turned, c * GROUPS + (n + 1))
                wait(act, p_ready, (c - 1) * UNITS + min(83 + 2 * n, UNITS))
                nc.scalar.copy(emb[:, g, :], turn_ps[:, n % 2, :])
                wait(act, parts_stored[n % 2], c * 80 + 16 * (n // 2))
                nc.scalar.copy(parts[:, n % 2, 0, :], turn_ps[:, n % 2, :]).then_inc(high_ready, 1)

            def middle(c, n):
                act.wait_ge(rest_ready, c * GROUPS + (n + 1))
                nc.scalar.copy(parts[:, n % 2, 1, :], rest[:, :]).then_inc(middle_ready, 1)

            def piece(k):
                cols = slice(PCOLS * k, PCOLS * (k + 1))
                units = slice(PCOLS // 2 * k, PCOLS // 2 * (k + 1))
                raw = w_raw[:, k % 2, :]
                raw_t = raw.rearrange("p (u h n) -> p u h n", h=2, n=P)
                rest_t = w_rest.rearrange("p (u h n) -> p u h n", h=2, n=P)
                fine_t = w_fine[:, units].rearrange("p (u n) -> p u n", n=P)
                act.wait_ge(raw_loaded[k % 2], 64 * (k // 2 + 1))
                nc.scalar.copy(w_main[:, cols], raw)
                nc.scalar.copy(fine_t[64:96], raw_t[64:96, :, 1, :]).then_inc(w_high, 1)
                act.wait_ge(w_rest_ready, k + 1)
                nc.scalar.copy(w_main[64:128, cols], w_rest[64:128, :])
                nc.scalar.copy(fine_t[32:64], rest_t[32:64, :, 0, :]).then_inc(w_middle, 1)

            def zout(c, k):
                act.wait_ge(summed, c * REDUCTIONS + min(PER_BLOCK * (k + 1), REDUCTIONS))
                if k == 0:
                    wait(act, h1_ready, c * M1)
                rows = ZLAST if k == ZBLOCKS - 1 else P
                nc.scalar.copy(z[0:rows, k, :], z_ps[0:rows, k % 2, :]).then_inc(z_out, 1)

            def mlp(c):
                for m in range(M1):
                    act.wait_ge(h1_ready, c * M1 + (m + 1))
                    if m == 0:
                        wait(act, y_stored, c * 16)
                    nc.scalar.activation(h1[:, m, :], t_ps[:, m, :], ACT.Relu,
                                         bias=b1_sb[:, m:m + 1]).then_inc(a1_ready, 1)
                for m in range(M2):
                    act.wait_ge(h2_ready, c * M2 + (m + 1))
                    nc.scalar.activation(h2[:, m, :], t_ps[:, m, :], ACT.Relu,
                                         bias=b2_sb[:, m:m + 1]).then_inc(a2_ready, 1)
                act.wait_ge(y_ready, c + 1)
                nc.scalar.copy(h1[0:1, 0, :], t_ps[0:1, 2, :]).then_inc(y_copied, 1)
                act.wait_ge(y_copied, c + 1)
                act.dma_start(out[c], h1[0:1, 0, :]).then_inc(y_stored, 16)

            act.wait_ge(consts_loaded, 16 * N_CONST)

            def body(c, order):
                for step, *a in order:
                    if step == "turn":
                        high(c + a[0], a[1])
                    elif step == "rest":
                        middle(c + a[0], a[1])
                    elif step == "piece":
                        piece(a[0])
                    elif step == "zout":
                        zout(c, a[0])
                    elif step == "mlp":
                        mlp(c)
            chunks(act, body)
            act.wait_ge(y_stored, 16 * CHUNKS)

        @block.vector
        def _(dve):
            def rest_of(c, n):
                g = GROUPS - 1 - n
                dve.wait_ge(high_ready, c * GROUPS + (n + 1))
                wait(dve, low_ready, c * GROUPS + n)
                nc.vector.tensor_tensor(rest[:, :], emb[:, g, :], parts[:, n % 2, 0, :],
                                        ALU.subtract).then_inc(rest_ready, 1)

            def low_of(c, n):
                dve.wait_ge(middle_ready, c * GROUPS + (n + 1))
                nc.vector.tensor_tensor(parts[:, n % 2, 2, :], rest[:, :], parts[:, n % 2, 1, :],
                                        ALU.subtract).then_inc(low_ready, 1)

            def piece(k):
                cols = slice(PCOLS * k, PCOLS * (k + 1))
                units = slice(PCOLS // 2 * k, PCOLS // 2 * (k + 1))
                main_t = w_main[:, cols].rearrange("p (u h n) -> p u h n", h=2, n=P)
                rest_t = w_rest.rearrange("p (u h n) -> p u h n", h=2, n=P)
                fine_t = w_fine[:, units].rearrange("p (u n) -> p u n", n=P)
                dve.wait_ge(w_high, k + 1)
                wait(dve, w_ready, k)
                nc.vector.tensor_tensor(w_rest, w_raw[:, k % 2, :], w_main[:, cols],
                                        ALU.subtract).then_inc(w_rest_ready, 1)
                nc.vector.tensor_copy(fine_t[0:32], main_t[0:32, :, 0, :])
                dve.wait_ge(w_middle, k + 1)
                nc.vector.tensor_tensor(fine_t[96:128], rest_t[96:128, :, 1, :], main_t[96:128, :, 1, :],
                                        ALU.subtract)
                nc.vector.tensor_tensor(fine_t[32:64], rest_t[32:64, :, 0, :], fine_t[32:64],
                                        ALU.subtract).then_inc(w_ready, 1)

            def unit(c, u):
                _, _, h, _ = unit_of(u)
                dve.wait_ge(t_ready, c * UNITS + (u + 1))
                if u >= PRODUCT_RING:
                    dve.wait_ge(summed, c * REDUCTIONS + (u // 2 - 1))
                elif u % 2 == 0:
                    wait(dve, summed, (c - 1) * REDUCTIONS + (REDUCTIONS - 1 + u // 2))
                slot, at = 2 * (u % 2), 2 * (u % PRODUCT_RING)
                second = emb[:, h:h + 1, :].broadcast_to([P, 2, CHUNK])
                nc.vector.tensor_tensor(prod[:, at:at + 2, :], t_ps[:, slot:slot + 2, :], second,
                                        ALU.mult).then_inc(p_ready, 1)

            def body(c, order):
                for step, *a in order:
                    if step == "rest":
                        rest_of(c + a[0], a[1])
                    elif step == "low":
                        low_of(c + a[0], a[1])
                    elif step == "piece":
                        piece(a[0])
                    elif step == "unit":
                        unit(c, a[0])
            chunks(dve, body)


def pair_number(i, j):
    return i * FIELDS - i * (i + 1) // 2 + (j - i - 1)


def tile_pairs():
    tiles = []
    for u in range(UNITS):
        _, g, h, v = unit_of(u)
        f, s = PER * g, PER * h
        if h != g:
            for half in range(2):
                i = f + 2 * v + half
                tiles.append([(pair_number(i, s + p), False) for p in range(PER)])
        else:
            tiles.append([None, (pair_number(f, f + 1), False), (pair_number(f, f + 2), False),
                          (pair_number(f + 2, f + 3), False)])
            tiles.append([(pair_number(f, f + 3), True), None, (pair_number(f + 1, f + 2), False),
                          (pair_number(f + 1, f + 3), False)])
    return tiles


def z_row(t, p):
    block, t = divmod(t, BATCH_TILES * PER_BLOCK)
    if block < ZBLOCKS - 1:
        return block, DIM * (t % BATCH_TILES) + PER * (t // BATCH_TILES) + p
    return block, PER * t + p


def kernel(**inputs):
    import numpy as np
    import concourse.bacc as bacc
    from concourse.bass_utils import run_bass_kernel_spmd

    a = {k: np.asarray(v) for k, v in inputs.items()}
    pairs = a["L0_rec_W"]
    turned = pairs.transpose(0, 2, 1)
    w_pairs = np.zeros((DIM, TILES, PER, DIM), np.float32)
    w1 = np.zeros((P, ZBLOCKS, H1), np.float32)
    for t, blocks in enumerate(tile_pairs()):
        for p, what in enumerate(blocks):
            if what is None:
                continue
            k, is_turned = what
            w_pairs[:, t, p, :] = turned[k] if is_turned else pairs[k]
            block, row = z_row(t, p)
            w1[row, block] = a["W_top1"][k]
    w1[ZLAST:ZLAST + DENSE, ZBLOCKS - 1] = a["W_top1"][-DENSE:]
    select = np.zeros((P, PER_BLOCK, DIM), np.float32)
    for r in range(PER_BLOCK):
        for p in range(PER):
            select[DIM * p:DIM * (p + 1), r, PER * r + p] = 1.0

    arrays = {
        "dense_t": np.ascontiguousarray(a["dense_ctx"].reshape(CHUNKS, CHUNK, DENSE).transpose(0, 2, 1)),
        "ids": np.ascontiguousarray(a["ids"].reshape(CHUNKS, BT, P, FIELDS).transpose(0, 2, 1, 3)),
        "w_pairs": w_pairs.reshape(DIM, TILES * P),
        "w1": w1,
        "b1": np.ascontiguousarray(a["b_top1"].reshape(M1, P).T),
        "w2": np.ascontiguousarray(a["W_top2"].reshape(M1, P, H2).transpose(1, 0, 2)),
        "b2": np.ascontiguousarray(a["b_top2"].reshape(M2, P).T),
        "w3": np.ascontiguousarray(a["W_top3"].reshape(M2, P).T),
        "select": select,
        "ident": np.eye(P, dtype=np.float32),
    }
    for f in range(FIELDS):
        arrays[f"tbl_{f}"] = np.ascontiguousarray(a[f"tbl_{f}"])

    nc = bacc.Bacc("TRN2", target_bir_lowering=False, num_devices=1)
    aps = {k: nc.dram_tensor(k, v.shape, mybir.dt.from_np(v.dtype), kind="ExternalInput").ap()
           for k, v in arrays.items()}
    out = nc.dram_tensor("y", (CHUNKS, 1, CHUNK), F32, kind="ExternalOutput").ap()
    tower(nc, aps["dense_t"], aps["ids"], [aps[f"tbl_{f}"] for f in range(FIELDS)], aps["w_pairs"], aps["w1"],
          aps["b1"], aps["w2"], aps["b2"], aps["w3"], aps["select"], aps["ident"], out)
    r = run_bass_kernel_spmd(nc, [arrays], core_ids=[0])
    return r.results[0]["y"].reshape(BATCH, 1)
```

```python
from contextlib import ExitStack

import concourse.bass as bass
from concourse import mybir
from concourse.alu_op_type import AluOpType as ALU

F32 = mybir.dt.float32
BF16 = mybir.dt.bfloat16
I32 = mybir.dt.int32
ACT = mybir.ActivationFunctionType

P = 128
FIELDS = 40
DIM = 32
PER = P // DIM
GROUPS = FIELDS // PER
BATCH = 2048
CHUNK = 512
CHUNKS = BATCH // CHUNK
BT = CHUNK // P
DENSE = 16
UNITS = GROUPS * GROUPS
TILES = 2 * UNITS
BATCH_TILES = 4
REDUCTIONS = TILES // BATCH_TILES
PER_BLOCK = P // (BATCH_TILES * PER)
ZBLOCKS = -(-REDUCTIONS // PER_BLOCK)
ZLAST = 2 * BATCH_TILES * PER
H1, H2 = 512, 256
M1, M2 = H1 // P, H2 // P

GATHER_RING = 5
STACK_RING = 5
RAW_RING = 5
PRODUCT_RING = 4
PIECE_UNITS = 4
PIECES = UNITS // PIECE_UNITS
PCOLS = 2 * P * PIECE_UNITS

X_TILE = ((0, 0), (1, 0), (2, 0), (3, 2))
Y_TILE = ((0, 3), (1, 1), (2, 1), (3, 1))


FIRST_PIECES = (2, 5, 5, 4, 4, 3, 2)
FIRST_PREPARED = (0, 0, 1, 4, 9, 16, 25, 36, 49, 63)
PREPARED = (5, 14, 24, 34, 45, 58)
AHEAD = (84, 87, 91, 96)


def unit_of(u):
    n = int(u ** 0.5)
    k = u - n * n
    g = GROUPS - 1 - n
    return n, g, GROUPS - 1 - k // 2, k % 2


def chunk_order(first, last):
    before = {u: [] for u in range(UNITS + 1)}

    def prepare(at, dc, n):
        for i, part in enumerate(("turn", "rest", "low")):
            before[at + i].append((part, dc, n))

    if first:
        pieces = iter(range(PIECES + 1))

        def weights(at, count):
            for k in [k for k in (next(pieces, None) for _ in range(count)) if k is not None]:
                if k < PIECES:
                    before[at].append(("begin", k))
                if k > 0:
                    before[at].append(("end", k - 1))

        weights(0, FIRST_PIECES[0])
        for n, at in enumerate(FIRST_PREPARED):
            for part in ("turn", "rest", "low"):
                before[at].append((part, 0, n))
            if n + 1 < len(FIRST_PIECES):
                count, behind = FIRST_PIECES[n + 1], max(FIRST_PREPARED[n + 1] - at, 1)
                for i in range(count):
                    weights(at + behind * i // count, 1)
        weights(FIRST_PREPARED[len(FIRST_PIECES) - 1] + 1, PIECES)
    else:
        for n, at in enumerate(PREPARED, 4):
            prepare(at, 0, n)
    if not last:
        for n, at in enumerate(AHEAD):
            prepare(at, 1, n)
    order = []
    for u in range(UNITS):
        order += before[u]
        order.append(("unit", u))
        if u % 2 == 1 and u >= 3:
            order.append(("sum", (u - 3) // 2))
        if u % 16 == 3 and u > 16:
            order.append(("zout", (u - 3) // 16 - 1))
    order += before[UNITS]
    order.append(("sum", REDUCTIONS - 1))
    order.append(("zout", ZBLOCKS - 1))
    order.append(("mlp", 0))
    return order


def tower(nc, dense_t, ids, tables, w_pairs, w1, b1, w2, b2, w3, select, ident, out):
    with ExitStack() as ctx:
        def sb(name, shape, dt):
            return ctx.enter_context(nc.sbuf_tensor(name, shape, dt))

        def ps(name, shape):
            return ctx.enter_context(nc.psum_tensor(name, shape, F32))

        def sem(name):
            return ctx.enter_context(nc.semaphore(name))

        w_main = sb("w_main", [P, TILES * P], BF16)
        w_fine = sb("w_fine", [P, UNITS * P], BF16)
        stack_main = sb("stack_main", [P, STACK_RING, PER, CHUNK], BF16)
        stack_fine = sb("stack_fine", [P, STACK_RING, PER // 2, CHUNK], BF16)
        gathered = sb("gathered", [P, GATHER_RING, BT, P], F32)
        emb = sb("emb", [P, GROUPS, CHUNK], F32)
        parts = sb("parts", [P, 2, 3, CHUNK], BF16)
        rest = sb("rest", [P, CHUNK], F32)
        prod = sb("prod", [P, 2 * PRODUCT_RING, CHUNK], F32)
        z = sb("z", [P, ZBLOCKS, CHUNK], F32)
        w1_sb = sb("w1_sb", [P, ZBLOCKS, H1], F32)
        w2_sb = sb("w2_sb", [P, M1, H2], F32)
        w3_sb = sb("w3_sb", [P, M2], F32)
        b1_sb = sb("b1_sb", [P, M1], F32)
        b2_sb = sb("b2_sb", [P, M2], F32)
        sel = sb("sel", [P, PER_BLOCK, DIM], F32)
        ident_sb = sb("ident_sb", [P, P], F32)
        idx = sb("idx", [P, 2, BT, FIELDS // 2], I32)
        shared = sb("shared", [P, 3 * PCOLS], F32)
        w_raw = ([shared[:, PCOLS * i:PCOLS * (i + 1)] for i in range(2)]
                 + [w1_sb[:, k:k + 2, :].rearrange("p k n -> p (k n)") for k in (0, 2, 4)])
        w_rest = [shared[:, 2 * PCOLS:3 * PCOLS],
                  z[:, ZBLOCKS - 3:ZBLOCKS - 1, :].rearrange("p k b -> p (k b)")]
        h1 = shared[:, 0:M1 * CHUNK].rearrange("p (m n) -> p m n", m=M1)
        h2 = shared[:, M1 * CHUNK:(M1 + M2) * CHUNK].rearrange("p (m n) -> p m n", m=M2)

        t_ps = ps("t_ps", [P, 4, CHUNK])
        turn_ps = ps("turn_ps", [P, 2, CHUNK])
        z_ps = ps("z_ps", [P, 2, CHUNK])

        parts_dram = nc.dram_tensor("parts_scratch", [2, 3, PER, DIM, CHUNK], BF16).ap()

        consts_loaded = sem("consts_loaded")
        ident_loaded = sem("ident_loaded")
        idx_loaded = [sem(f"idx_loaded{i}") for i in range(2)]
        gather_done = [sem(f"gather_done{i}") for i in range(GATHER_RING)]
        turned = sem("turned")
        high_ready = sem("high_ready")
        rest_ready = sem("rest_ready")
        middle_ready = sem("middle_ready")
        low_ready = sem("low_ready")
        parts_stored = [sem(f"parts_stored{i}") for i in range(2)]
        stacked = [sem(f"stacked{i}") for i in range(STACK_RING)]
        t_ready = sem("t_ready")
        p_ready = sem("p_ready")
        summed = sem("summed")
        z_out = sem("z_out")
        dense_loaded = sem("dense_loaded")
        raw_loaded = [sem(f"raw_loaded{i}") for i in range(RAW_RING)]
        w1_loaded = sem("w1_loaded")
        w_high = sem("w_high")
        w_rest_ready = sem("w_rest_ready")
        w_middle = sem("w_middle")
        w_cast = sem("w_cast")
        w_ready = sem("w_ready")
        h1_ready = sem("h1_ready")
        a1_ready = sem("a1_ready")
        h2_ready = sem("h2_ready")
        a2_ready = sem("a2_ready")
        y_ready = sem("y_ready")
        y_copied = sem("y_copied")
        y_stored = sem("y_stored")

        passed = [sem("passed_sp"), sem("passed_pool")]

        N_CONST = 5

        def wait(eng, s, value):
            if not (isinstance(value, int) and value <= 0):
                eng.wait_ge(s, value)

        def wait_alone(eng, s, value):
            wait(eng, s, value)
            if not isinstance(value, int):
                eng.sem_inc(passed[0] if eng is nc.sync else passed[1], 1)

        def chunks(eng, body):
            body(0, chunk_order(True, False))
            with eng.Fori(1, CHUNKS - 1) as c:
                body(c, chunk_order(False, False))
            body(CHUNKS - 1, chunk_order(False, True))

        block = ctx.enter_context(nc.Block())

        @block.sync
        def _(sp):
            def load_piece(k):
                wait_alone(sp, w_rest_ready, k - RAW_RING + 1)
                src = w_pairs[:, PCOLS * k:PCOLS * (k + 1)].rearrange("(o e) n -> o e n", o=1)
                sp.dma_start(w_raw[k % RAW_RING], src.broadcast_to([PER, DIM, PCOLS])).then_inc(raw_loaded[k % RAW_RING], 16)

            def load_idx(c, half):
                lo = (1 - half) * (FIELDS // 2)
                sp.dma_start(idx[:, half], ids[c, :, :, lo:lo + FIELDS // 2]).then_inc(idx_loaded[half], 16)

            def stack(c, n):
                ring, par = n % STACK_RING, n % 2
                wait_alone(sp, low_ready, c * GROUPS + (n + 1))
                m = n - 2
                if m >= 0 or not isinstance(c, int) or c > 0:
                    cc, mm = (c, m) if m >= 0 else (c - 1, m + GROUPS)
                    wait_alone(sp, stacked[mm % STACK_RING], cc * 256 + 128 * (mm // STACK_RING + 1))
                sp.dma_start(parts_dram[par].rearrange("k q e b -> (q e) k b"),
                             parts[:, par]).then_inc(parts_stored[par], 16)
                wait_alone(sp, parts_stored[par], c * 80 + 16 * (n // 2 + 1))
                if n >= STACK_RING:
                    wait_alone(sp, t_ready, c * UNITS + (n - STACK_RING + 1) ** 2)
                else:
                    wait_alone(sp, t_ready, (c - 1) * UNITS + (n + STACK_RING + 1) ** 2)
                for s, k in enumerate((0, 1, 0, 1)):
                    sp.dma_start(stack_main[DIM * s:DIM * (s + 1), ring],
                                 parts_dram[par, k].rearrange("q e b -> e q b")).then_inc(stacked[ring], 16)
                for half in range(2):
                    src = parts_dram[par].rearrange("k (v h) e b -> k h e v b", h=2)
                    for s, k in enumerate((2, 0)):
                        row = 64 * half + DIM * s
                        sp.dma_start(stack_fine[row:row + DIM, ring], src[k, half]).then_inc(stacked[ring], 16)

            load_idx(0, 0)
            sp.dma_start(ident_sb[:, :], ident).then_inc(ident_loaded, 16)
            for k in range(RAW_RING):
                load_piece(k)
            load_idx(0, 1)
            sp.dma_start(sel[:, :, :], select).then_inc(consts_loaded, 16)
            sp.dma_start(w2_sb[:, :, :], w2).then_inc(consts_loaded, 16)
            sp.dma_start(w3_sb[:, :], w3).then_inc(consts_loaded, 16)
            sp.dma_start(b1_sb[:, :], b1).then_inc(consts_loaded, 16)
            sp.dma_start(b2_sb[:, :], b2).then_inc(consts_loaded, 16)

            def body(c, order):
                for step, *a in order:
                    if step == "begin" and a[0] + RAW_RING < PIECES:
                        load_piece(a[0] + RAW_RING)
                    if step == "end" and a[0] == PIECES - 1:
                        sp.wait_ge(w_rest_ready, PIECES)
                        sp.dma_start(w1_sb[:, :, :], w1).then_inc(w1_loaded, 16)
                    if step == "low":
                        dc, n = a
                        stack(c + dc, n)
                        if dc == 1 and n == 0:
                            load_idx(c + 1, 1)
                        if dc == 0 and n == 5:
                            wait_alone(sp, h1_ready, c * M1)
                            sp.dma_start(z[ZLAST:ZLAST + DENSE, ZBLOCKS - 1, :],
                                         dense_t[c]).then_inc(dense_loaded, 16)
                            if order[-2] and ("turn", 1, 0) in order:
                                load_idx(c + 1, 0)
            chunks(sp, body)

        @block.gpsimd
        def _(pool):
            def gather(c, n):
                g, ring, half = GROUPS - 1 - n, n % GATHER_RING, n // GATHER_RING
                if n % GATHER_RING == 0:
                    wait_alone(pool, idx_loaded[half], c * 16 + 16)
                wait_alone(pool, turned, c * GROUPS + (n - GATHER_RING + 1))
                for t in range(BT):
                    for q in range(PER):
                        f = PER * g + q
                        col = f - (1 - half) * (FIELDS // 2)
                        nc.gpsimd.indirect_dma_start(
                            gathered[:, ring, t, DIM * q:DIM * (q + 1)], None, tables[f],
                            bass.IndirectOffsetOnAxis(ap=idx[:, half, t, col:col + 1], axis=0),
                        ).then_inc(gather_done[ring], 16)

            for n in range(GROUPS):
                gather(0, n)
            with pool.Fori(1, CHUNKS) as c:
                for n in range(GROUPS):
                    gather(c, n)

        @block.tensor
        def _(pe):
            def turn(c, n):
                ring = n % GATHER_RING
                uses = 2 if GROUPS == 2 * GATHER_RING else 1
                pe.wait_ge(gather_done[ring], c * (uses * 256) + 256 * (n // GATHER_RING + 1))
                wait(pe, high_ready, c * GROUPS + (n - 1))
                for t in range(BT):
                    last = nc.tensor.transpose(turn_ps[:, n % 2, P * t:P * (t + 1)],
                                               gathered[:, ring, t, :], ident_sb[:, :])
                last.then_inc(turned, 1)

            def main(out_ap, tile, cols, ring, q):
                nc.tensor.matmul(out_ap, w_main[:, P * tile + cols.start:P * tile + cols.stop],
                                 stack_main[:, ring, q, :], start=True, stop=False)

            def fine(out_ap, u, half, cols, ring, q):
                rows = slice(64 * half, 64 * half + 64)
                return nc.tensor.matmul(out_ap, w_fine[rows, P * u + cols.start:P * u + cols.stop],
                                        stack_fine[rows, ring, q // 2, :], start=False, stop=True)

            def unit(c, u, first):
                n, g, h, v = unit_of(u)
                ring, slot = n % STACK_RING, 2 * (u % 2)
                if u == n * n:
                    pe.wait_ge(stacked[ring], c * 256 + 128 * (n // STACK_RING + 1))
                if first and u % PIECE_UNITS == 0:
                    pe.wait_ge(w_ready, u // PIECE_UNITS + 1)
                if u >= 2:
                    wait(pe, p_ready, c * UNITS + (u - 1))
                elif u == 0:
                    wait(pe, a2_ready, c * M2)
                else:
                    wait(pe, y_copied, c)
                if h != g:
                    for half in range(2):
                        main(t_ps[:, slot + half, :], 2 * u + half, slice(0, P), ring, 2 * v + half)
                    for half in range(2):
                        last = fine(t_ps[:, slot + half, :], u, half, slice(0, P), ring, 2 * v + half)
                else:
                    for half, blocks in enumerate((X_TILE, Y_TILE)):
                        for p, q in blocks:
                            cols = slice(DIM * p, DIM * (p + 1))
                            main(t_ps[cols, slot + half, :], 2 * u + half, cols, ring, q)
                        for p, q in blocks:
                            cols = slice(DIM * p, DIM * (p + 1))
                            last = fine(t_ps[cols, slot + half, :], u, half, cols, ring, q)
                last.then_inc(t_ready, 1)

            def sum_pairs(c, b):
                if b == 0:
                    pe.wait_ge(consts_loaded, 16 * N_CONST)
                k, r = b // PER_BLOCK, b % PER_BLOCK
                pe.wait_ge(p_ready, c * UNITS + (2 * b + 2))
                if r == 0 and k >= 2:
                    pe.wait_ge(z_out, c * ZBLOCKS + (k - 1))
                for j in range(BATCH_TILES):
                    at = (BATCH_TILES * b + j) % (2 * PRODUCT_RING)
                    if k < ZBLOCKS - 1:
                        rows, which, start, stop = slice(DIM * j, DIM * (j + 1)), r, r == 0, r == PER_BLOCK - 1
                    else:
                        which = BATCH_TILES * r + j
                        rows, start, stop = slice(0, DIM), which == 0, which == PER_BLOCK - 1
                    last = nc.tensor.matmul(z_ps[rows, k % 2, :], sel[:, which, :], prod[:, at, :],
                                            start=start, stop=stop)
                last.then_inc(summed, 1)

            def mlp(c):
                pe.wait_ge(p_ready, c * UNITS + UNITS)
                pe.wait_ge(w1_loaded, 16)
                for k in range(ZBLOCKS):
                    rows = P
                    if k == ZBLOCKS - 2:
                        pe.wait_ge(z_out, c * ZBLOCKS + (ZBLOCKS - 1))
                    elif k == ZBLOCKS - 1:
                        rows = ZLAST + DENSE
                        pe.wait_ge(z_out, c * ZBLOCKS + ZBLOCKS)
                        pe.wait_ge(dense_loaded, c * 16 + 16)
                    elif k == 0:
                        pe.wait_ge(z_out, c * ZBLOCKS + (ZBLOCKS - 2))
                    for m in range(M1):
                        last = nc.tensor.matmul(t_ps[:, m, :], w1_sb[0:rows, k, P * m:P * (m + 1)],
                                                z[0:rows, k, :], start=(k == 0), stop=(k == ZBLOCKS - 1))
                        if k == ZBLOCKS - 1:
                            last.then_inc(h1_ready, 1)
                pe.wait_ge(a1_ready, c * M1 + M1)
                for m in range(M2):
                    for k in range(M1):
                        last = nc.tensor.matmul(t_ps[:, m, :], w2_sb[:, k, P * m:P * (m + 1)], h1[:, k, :],
                                                start=(k == 0), stop=(k == M1 - 1))
                    last.then_inc(h2_ready, 1)
                pe.wait_ge(a2_ready, c * M2 + M2)
                for k in range(M2):
                    last = nc.tensor.matmul(t_ps[0:1, 2, :], w3_sb[:, k:k + 1], h2[:, k, :],
                                            start=(k == 0), stop=(k == M2 - 1))
                last.then_inc(y_ready, 1)

            pe.wait_ge(ident_loaded, 16)

            def body(c, order):
                for step, *a in order:
                    if step == "turn":
                        turn(c + a[0], a[1])
                    elif step == "unit":
                        unit(c, a[0], isinstance(c, int) and c == 0)
                    elif step == "sum":
                        sum_pairs(c, a[0])
                    elif step == "mlp":
                        mlp(c)
            chunks(pe, body)

        @block.scalar
        def _(act):
            def high(c, n):
                g = GROUPS - 1 - n
                act.wait_ge(turned, c * GROUPS + (n + 1))
                wait(act, p_ready, (c - 1) * UNITS + min(83 + 2 * n, UNITS))
                nc.scalar.copy(emb[:, g, :], turn_ps[:, n % 2, :])
                wait(act, parts_stored[n % 2], c * 80 + 16 * (n // 2))
                nc.scalar.copy(parts[:, n % 2, 0, :], turn_ps[:, n % 2, :]).then_inc(high_ready, 1)

            def middle(c, n):
                act.wait_ge(rest_ready, c * GROUPS + (n + 1))
                nc.scalar.copy(parts[:, n % 2, 1, :], rest[:, :]).then_inc(middle_ready, 1)

            def begin_piece(k):
                raw = w_raw[k % RAW_RING]
                raw_t = raw.rearrange("p (u h n) -> p u h n", h=2, n=P)
                fine_t = w_fine[:, PCOLS // 2 * k:PCOLS // 2 * (k + 1)].rearrange("p (u n) -> p u n", n=P)
                act.wait_ge(raw_loaded[k % RAW_RING], 16 * (k // RAW_RING + 1))
                nc.scalar.copy(w_main[:, PCOLS * k:PCOLS * (k + 1)], raw)
                nc.scalar.copy(fine_t[0:32], raw_t[0:32, :, 0, :])
                nc.scalar.copy(fine_t[64:96], raw_t[64:96, :, 1, :]).then_inc(w_high, 1)

            def end_piece(k):
                act.wait_ge(w_rest_ready, k + 1)
                nc.scalar.copy(w_main[64:128, PCOLS * k:PCOLS * (k + 1)], w_rest[k % 2][64:128, :]).then_inc(w_middle, 1)

            def zout(c, k):
                act.wait_ge(summed, c * REDUCTIONS + min(PER_BLOCK * (k + 1), REDUCTIONS))
                if k == 0:
                    wait(act, h1_ready, c * M1)
                rows = ZLAST if k == ZBLOCKS - 1 else P
                nc.scalar.copy(z[0:rows, k, :], z_ps[0:rows, k % 2, :]).then_inc(z_out, 1)

            def mlp(c):
                act.wait_ge(consts_loaded, 16 * N_CONST)
                for m in range(M1):
                    act.wait_ge(h1_ready, c * M1 + (m + 1))
                    if m == 0:
                        wait(act, y_stored, c * 16)
                    nc.scalar.activation(h1[:, m, :], t_ps[:, m, :], ACT.Relu,
                                         bias=b1_sb[:, m:m + 1]).then_inc(a1_ready, 1)
                for m in range(M2):
                    act.wait_ge(h2_ready, c * M2 + (m + 1))
                    nc.scalar.activation(h2[:, m, :], t_ps[:, m, :], ACT.Relu,
                                         bias=b2_sb[:, m:m + 1]).then_inc(a2_ready, 1)
                act.wait_ge(y_ready, c + 1)
                nc.scalar.copy(h1[0:1, 0, :], t_ps[0:1, 2, :]).then_inc(y_copied, 1)
                act.wait_ge(y_copied, c + 1)
                act.dma_start(out[c], h1[0:1, 0, :]).then_inc(y_stored, 16)


            def body(c, order):
                for step, *a in order:
                    if step == "turn":
                        high(c + a[0], a[1])
                    elif step == "rest":
                        middle(c + a[0], a[1])
                    elif step == "begin":
                        begin_piece(a[0])
                    elif step == "end":
                        end_piece(a[0])
                    elif step == "zout":
                        zout(c, a[0])
                    elif step == "mlp":
                        mlp(c)
            chunks(act, body)
            act.wait_ge(y_stored, 16 * CHUNKS)

        @block.vector
        def _(dve):
            def rest_of(c, n):
                g = GROUPS - 1 - n
                dve.wait_ge(high_ready, c * GROUPS + (n + 1))
                wait(dve, low_ready, c * GROUPS + n)
                nc.vector.tensor_tensor(rest[:, :], emb[:, g, :], parts[:, n % 2, 0, :],
                                        ALU.subtract).then_inc(rest_ready, 1)

            def low_of(c, n):
                dve.wait_ge(middle_ready, c * GROUPS + (n + 1))
                nc.vector.tensor_tensor(parts[:, n % 2, 2, :], rest[:, :], parts[:, n % 2, 1, :],
                                        ALU.subtract).then_inc(low_ready, 1)

            def views(k):
                cols, units = slice(PCOLS * k, PCOLS * (k + 1)), slice(PCOLS // 2 * k, PCOLS // 2 * (k + 1))
                return (w_main[:, cols].rearrange("p (u h n) -> p u h n", h=2, n=P),
                        w_rest[k % 2].rearrange("p (u h n) -> p u h n", h=2, n=P),
                        w_fine[:, units].rearrange("p (u n) -> p u n", n=P))

            def begin_piece(k):
                main_t, _, fine_t = views(k)
                dve.wait_ge(w_high, k + 1)
                wait(dve, w_ready, k - 1)
                nc.vector.tensor_tensor(w_rest[k % 2], w_raw[k % RAW_RING], w_main[:, PCOLS * k:PCOLS * (k + 1)],
                                        ALU.subtract).then_inc(w_rest_ready, 1)

            def end_piece(k):
                main_t, rest_t, fine_t = views(k)
                dve.wait_ge(w_rest_ready, k + 1)
                nc.vector.tensor_copy(fine_t[32:64], rest_t[32:64, :, 0, :]).then_inc(w_cast, 1)
                dve.wait_ge(w_middle, k + 1)
                nc.vector.tensor_tensor(fine_t[96:128], rest_t[96:128, :, 1, :], main_t[96:128, :, 1, :],
                                        ALU.subtract)
                dve.wait_ge(w_cast, k + 1)
                nc.vector.tensor_tensor(fine_t[32:64], rest_t[32:64, :, 0, :], fine_t[32:64],
                                        ALU.subtract).then_inc(w_ready, 1)

            def unit(c, u):
                _, _, h, _ = unit_of(u)
                dve.wait_ge(t_ready, c * UNITS + (u + 1))
                if u >= PRODUCT_RING:
                    dve.wait_ge(summed, c * REDUCTIONS + (u // 2 - 1))
                elif u % 2 == 0:
                    wait(dve, summed, (c - 1) * REDUCTIONS + (REDUCTIONS - 1 + u // 2))
                slot, at = 2 * (u % 2), 2 * (u % PRODUCT_RING)
                second = emb[:, h:h + 1, :].broadcast_to([P, 2, CHUNK])
                nc.vector.tensor_tensor(prod[:, at:at + 2, :], t_ps[:, slot:slot + 2, :], second,
                                        ALU.mult).then_inc(p_ready, 1)

            def body(c, order):
                for step, *a in order:
                    if step == "rest":
                        rest_of(c + a[0], a[1])
                    elif step == "low":
                        low_of(c + a[0], a[1])
                    elif step == "begin":
                        begin_piece(a[0])
                    elif step == "end":
                        end_piece(a[0])
                    elif step == "unit":
                        unit(c, a[0])
            chunks(dve, body)


def pair_number(i, j):
    return i * FIELDS - i * (i + 1) // 2 + (j - i - 1)


def tile_pairs():
    tiles = []
    for u in range(UNITS):
        _, g, h, v = unit_of(u)
        f, s = PER * g, PER * h
        if h != g:
            for half in range(2):
                i = f + 2 * v + half
                tiles.append([(pair_number(i, s + p), False) for p in range(PER)])
        else:
            tiles.append([None, (pair_number(f, f + 1), False), (pair_number(f, f + 2), False),
                          (pair_number(f + 2, f + 3), False)])
            tiles.append([(pair_number(f, f + 3), True), None, (pair_number(f + 1, f + 2), False),
                          (pair_number(f + 1, f + 3), False)])
    return tiles


def z_row(t, p):
    block, t = divmod(t, BATCH_TILES * PER_BLOCK)
    if block < ZBLOCKS - 1:
        return block, DIM * (t % BATCH_TILES) + PER * (t // BATCH_TILES) + p
    return block, PER * t + p


def kernel(**inputs):
    import numpy as np
    import concourse.bacc as bacc
    from concourse.bass_utils import run_bass_kernel_spmd

    a = {k: np.asarray(v) for k, v in inputs.items()}
    pairs = a["L0_rec_W"]
    turned = pairs.transpose(0, 2, 1)
    w_pairs = np.zeros((DIM, TILES, PER, DIM), np.float32)
    w1 = np.zeros((P, ZBLOCKS, H1), np.float32)
    for t, blocks in enumerate(tile_pairs()):
        for p, what in enumerate(blocks):
            if what is None:
                continue
            k, is_turned = what
            w_pairs[:, t, p, :] = turned[k] if is_turned else pairs[k]
            block, row = z_row(t, p)
            w1[row, block] = a["W_top1"][k]
    w1[ZLAST:ZLAST + DENSE, ZBLOCKS - 1] = a["W_top1"][-DENSE:]
    select = np.zeros((P, PER_BLOCK, DIM), np.float32)
    for r in range(PER_BLOCK):
        for p in range(PER):
            select[DIM * p:DIM * (p + 1), r, PER * r + p] = 1.0

    arrays = {
        "dense_t": np.ascontiguousarray(a["dense_ctx"].reshape(CHUNKS, CHUNK, DENSE).transpose(0, 2, 1)),
        "ids": np.ascontiguousarray(a["ids"].reshape(CHUNKS, BT, P, FIELDS).transpose(0, 2, 1, 3)),
        "w_pairs": w_pairs.reshape(DIM, TILES * P),
        "w1": w1,
        "b1": np.ascontiguousarray(a["b_top1"].reshape(M1, P).T),
        "w2": np.ascontiguousarray(a["W_top2"].reshape(M1, P, H2).transpose(1, 0, 2)),
        "b2": np.ascontiguousarray(a["b_top2"].reshape(M2, P).T),
        "w3": np.ascontiguousarray(a["W_top3"].reshape(M2, P).T),
        "select": select,
        "ident": np.eye(P, dtype=np.float32),
    }
    for f in range(FIELDS):
        arrays[f"tbl_{f}"] = np.ascontiguousarray(a[f"tbl_{f}"])

    nc = bacc.Bacc("TRN2", target_bir_lowering=False, num_devices=1)
    aps = {k: nc.dram_tensor(k, v.shape, mybir.dt.from_np(v.dtype), kind="ExternalInput").ap()
           for k, v in arrays.items()}
    out = nc.dram_tensor("y", (CHUNKS, 1, CHUNK), F32, kind="ExternalOutput").ap()
    tower(nc, aps["dense_t"], aps["ids"], [aps[f"tbl_{f}"] for f in range(FIELDS)], aps["w_pairs"], aps["w1"],
          aps["b1"], aps["w2"], aps["b2"], aps["w3"], aps["select"], aps["ident"], out)
    r = run_bass_kernel_spmd(nc, [arrays], core_ids=[0])
    return r.results[0]["y"].reshape(BATCH, 1)
```

```python
from contextlib import ExitStack

import concourse.bass as bass
from concourse import mybir
from concourse.alu_op_type import AluOpType as ALU

F32 = mybir.dt.float32
BF16 = mybir.dt.bfloat16
I32 = mybir.dt.int32
ACT = mybir.ActivationFunctionType

P = 128
FIELDS = 40
DIM = 32
PER = P // DIM
GROUPS = FIELDS // PER
BATCH = 2048
CHUNK = 512
CHUNKS = BATCH // CHUNK
BT = CHUNK // P
DENSE = 16
UNITS = GROUPS * GROUPS
TILES = 2 * UNITS
BATCH_TILES = 4
REDUCTIONS = TILES // BATCH_TILES
PER_BLOCK = P // (BATCH_TILES * PER)
ZBLOCKS = -(-REDUCTIONS // PER_BLOCK)
ZDENSE = REDUCTIONS % PER_BLOCK * PER
H1, H2 = 512, 256
M1, M2 = H1 // P, H2 // P

HOT_STEPS = 2
HOT_BLOCKS = 10
HOT_RING = 6

GATHER_RING = 5
T_RING = 3
STACK_RING = 5
PRODUCT_RING = 4
PIECE_UNITS = 20
PIECES = UNITS // PIECE_UNITS
HCOLS = P * PIECE_UNITS
PCOLS = 2 * HCOLS
WCOLS = PCOLS // PER

X_TILE = ((0, 0), (1, 0), (2, 0), (3, 2))
Y_TILE = ((0, 3), (1, 1), (2, 1), (3, 1))


FIRST_PREPARED = (0, 0, 0, 1, 6, 14, 24, 34, 46, 60)
PREPARED = (1, 4, 5, 14, 24, 34, 45, 58)
AHEAD = (82, 88)
SPLIT = (0, 5, 17, 29)
MLP_BEHIND = 4


def main_tile(u, half):
    quarter, at = divmod(u, PIECE_UNITS // PER)
    return (2 * quarter + half) * (PIECE_UNITS // PER) + at


def one_hot(rows):
    hot = []
    for n in range(HOT_STEPS):
        for q in range(PER):
            f = PER * (GROUPS - 1 - n) + q
            blocks = -(-rows[f] // P)
            if blocks <= HOT_BLOCKS and rows[f] % blocks == 0:
                hot.append((n, q, f, blocks))
    return hot


def unit_of(u):
    n = int(u ** 0.5)
    k = u - n * n
    g = GROUPS - 1 - n
    return n, g, GROUPS - 1 - k // 2, k % 2


def t_slot(u, first):
    return (u if first or u >= MLP_BEHIND else u + 1) % T_RING


def chunk_order(first, last):
    before = {u: [] for u in range(UNITS + 1)}

    def prepare(at, dc, n, spread=True):
        for i, part in enumerate(("turn", "rest", "low")):
            before[at + i * spread].append((part, dc, n))

    if first:
        before[0] += [("hot", 0, 0), ("hot", 0, 1), ("split", 0)]
        for n, at in enumerate(FIRST_PREPARED):
            if n + 1 < HOT_STEPS:
                before[at] += [("turn", 0, n), ("hot", n + 1, 0), ("rest", 0, n), ("low", 0, n)]
                if n == 0:
                    before[at].append(("lows", 0))
                before[at].append(("hot", n + 1, 1))
            else:
                prepare(at, 0, n, spread=n > 3)
        for k, at in enumerate(SPLIT, 1):
            before[at].append(("split", k))
            before[at + (at > 0)].append(("lows", k))
    else:
        for n, at in enumerate(PREPARED, len(AHEAD)):
            if at != MLP_BEHIND:
                prepare(at, 0, n)
    if not last:
        for n, at in enumerate(AHEAD):
            prepare(at, 1, n)
    order = []
    for u in range(UNITS):
        order += before[u]
        order.append(("unit", u))
        if u % 2 == 1 and u >= 3:
            order.append(("sum", 0, (u - 3) // 2))
        if u % (2 * PER_BLOCK) == 1 and u > 1:
            order.append(("zout", 0, u // (2 * PER_BLOCK) - 1))
        if not first:
            if u == 1:
                order += [("sum", -1, REDUCTIONS - 1), ("zout", -1, ZBLOCKS - 1)]
            if u == MLP_BEHIND - 1:
                n = len(AHEAD) + PREPARED.index(MLP_BEHIND)
                order += [("layer1", -1), ("turn", 0, n), ("rest", 0, n), ("low", 0, n), ("layers23", -1)]
    order += before[UNITS]
    if last:
        order += [("sum", 0, REDUCTIONS - 1), ("zout", 0, ZBLOCKS - 1), ("layer1", 0), ("layers23", 0)]
    return order


def tower(nc, dense_t, ids, hot_ids, hot_rows, tables, w_pairs, w1, b1, w2, b2, w3, select, ident, out):
    with ExitStack() as ctx:
        def sb(name, shape, dt):
            return ctx.enter_context(nc.sbuf_tensor(name, shape, dt))

        def ps(name, shape):
            return ctx.enter_context(nc.psum_tensor(name, shape, F32))

        def sem(name):
            return ctx.enter_context(nc.semaphore(name))

        w_main = sb("w_main", [P, TILES * P], BF16)
        w_fine = sb("w_fine", [P, UNITS * P], BF16)
        stack_main = sb("stack_main", [P, STACK_RING, PER, CHUNK], BF16)
        stack_fine = sb("stack_fine", [P, STACK_RING, PER // 2, CHUNK], BF16)
        gathered = sb("gathered", [P, GATHER_RING, BT, P], F32)
        emb = sb("emb", [P, GROUPS, CHUNK], F32)
        parts = sb("parts", [P, 2, 3, CHUNK], BF16)
        rest = sb("rest", [P, CHUNK], F32)
        prod = sb("prod", [P, 2 * PRODUCT_RING, CHUNK], F32)
        z = sb("z", [P, ZBLOCKS, CHUNK], F32)
        w1_sb = sb("w1_sb", [P, ZBLOCKS, H1], F32)
        w2_sb = sb("w2_sb", [P, M1, H2], F32)
        w3_sb = sb("w3_sb", [P, M2], F32)
        b1_sb = sb("b1_sb", [P, M1], F32)
        b2_sb = sb("b2_sb", [P, M2], F32)
        sel = sb("sel", [P, PER_BLOCK, DIM], F32)
        ident_sb = sb("ident_sb", [P, P], F32)
        idx = sb("idx", [P, 2, BT, FIELDS // 2], I32)
        shared = sb("shared", [P, (M1 + M2) * CHUNK], F32)
        w_raw, w_rest = (shared[:, WCOLS * i:WCOLS * (i + 1)] for i in range(2))
        w_parts = z[:, :, :].rearrange("p k b -> p (k b)")[:, ZBLOCKS * CHUNK - 3 * WCOLS // 2:].bitcast(BF16)
        w_parts = w_parts.rearrange("p (k n) -> p k n", k=3)
        h1 = shared[:, 0:M1 * CHUNK].rearrange("p (m n) -> p m n", m=M1)
        h2 = shared[:, M1 * CHUNK:(M1 + M2) * CHUNK].rearrange("p (m n) -> p m n", m=M2)

        hot = one_hot([t.shape[0] for t in tables])
        hot_idx = [w1_sb[:, i, :].bitcast(I32) for i in range(len(hot))]
        flat_prod = prod[:, :, :].rearrange("p k n -> p (k n)")
        hot_table = [flat_prod[:, DIM * HOT_BLOCKS * i:DIM * HOT_BLOCKS * (i + 1)] for i in range(len(hot))]
        one_hots = emb[:, 0:HOT_RING, :]
        hot_row = sb("hot_row", [P, len(hot) * HOT_BLOCKS], F32)

        t_ps = ps("t_ps", [P, 2 * T_RING, CHUNK])
        turn_ps = ps("turn_ps", [P, CHUNK])
        z_ps = ps("z_ps", [P, CHUNK])

        parts_dram = nc.dram_tensor("parts_scratch", [2, 3, PER, DIM, CHUNK], BF16).ap()

        consts_loaded = sem("consts_loaded")
        ident_loaded = sem("ident_loaded")
        idx_loaded = [sem(f"idx_loaded{i}") for i in range(2)]
        hot_loaded = [sem(f"hot_loaded{n}") for n in range(HOT_STEPS)]
        hot_ready = sem("hot_ready")
        hot_used = sem("hot_used")
        w1_loaded = sem("w1_loaded")
        gather_done = [sem(f"gather_done{i}") for i in range(GATHER_RING)]
        turned = sem("turned")
        high_ready = sem("high_ready")
        rest_ready = sem("rest_ready")
        middle_ready = sem("middle_ready")
        low_ready = sem("low_ready")
        parts_stored = [sem(f"parts_stored{i}") for i in range(2)]
        stacked = [sem(f"stacked{i}") for i in range(STACK_RING)]
        t_ready = sem("t_ready")
        p_ready = sem("p_ready")
        summed = sem("summed")
        z_out = sem("z_out")
        dense_loaded = sem("dense_loaded")
        raw_loaded = sem("raw_loaded")
        w_high = sem("w_high")
        w_rest_ready = sem("w_rest_ready")
        w_middle = sem("w_middle")
        w_low = sem("w_low")
        w_loaded = [sem(f"w_loaded{i}") for i in range(PIECES)]
        h1_ready = sem("h1_ready")
        a1_ready = sem("a1_ready")
        h2_ready = sem("h2_ready")
        a2_ready = sem("a2_ready")
        y_ready = sem("y_ready")
        y_copied = sem("y_copied")
        y_stored = sem("y_stored")

        passed = [sem("passed_sp"), sem("passed_pool")]

        N_CONST = 5

        def hots(n):
            rounds = [(m, b, i) for m in range(HOT_STEPS) for b in range(HOT_BLOCKS)
                      for i, (step, _, _, blocks) in enumerate(hot) if step == m and b < blocks]
            return [(k, b, i) for k, (m, b, i) in enumerate(rounds) if m == n]

        def hot_loads(n):
            return 16 * (2 * sum(m == n for m, _, _, _ in hot) + (n == 0))

        HOTS = sum(blocks for _, _, _, blocks in hot)

        def is_first(c):
            return isinstance(c, int) and c == 0

        def gathered_fields(c, n):
            small = [q for m, q, _, _ in hot if m == n] if is_first(c) else []
            return [q for q in range(PER) if q not in small]

        def gathers(c, n):
            ring = n % GATHER_RING
            spared = sum(16 * BT for m, _, _, _ in hot if m % GATHER_RING == ring)
            return c * (GROUPS // GATHER_RING * 256) + 256 * (n // GATHER_RING + 1) - spared

        def wait(eng, s, value):
            if not (isinstance(value, int) and value <= 0):
                eng.wait_ge(s, value)

        def wait_alone(eng, s, value):
            wait(eng, s, value)
            if not isinstance(value, int):
                eng.sem_inc(passed[0] if eng is nc.sync else passed[1], 1)

        def mlp_banks(units):
            slots = [t_slot(u, False) for u in range(units - T_RING, units)]
            return [2 * slot + half for slot in slots for half in range(2)]

        def chunks(eng, body):
            body(0, chunk_order(True, False))
            with eng.Fori(1, CHUNKS - 1) as c:
                body(c, chunk_order(False, False))
            body(CHUNKS - 1, chunk_order(False, True))

        block = ctx.enter_context(nc.Block())

        @block.sync
        def _(sp):
            def load_raw(k):
                wait(sp, w_rest_ready, k)
                sp.dma_start(w_raw, w_pairs[k]).then_inc(raw_loaded, 16)

            def spread_piece(k):
                sp.wait_ge(w_low, k + 1)
                for s, part in enumerate((0, 0, 1, 1)):
                    sp.dma_start(w_main[DIM * s:DIM * (s + 1), PCOLS * k:PCOLS * (k + 1)],
                                 w_parts[:, part, :]).then_inc(w_loaded[k], 16)
                for half in range(2):
                    for s, part in enumerate((0, 2)):
                        row = 64 * half + DIM * s
                        sp.dma_start(w_fine[row:row + DIM, HCOLS * k:HCOLS * (k + 1)],
                                     w_parts[:, part, WCOLS // 2 * half:WCOLS // 2 * (half + 1)],
                                     ).then_inc(w_loaded[k], 16)

            def load_idx(c, half):
                lo = (1 - half) * (FIELDS // 2)
                sp.dma_start(idx[:, half], ids[c, :, :, lo:lo + FIELDS // 2]).then_inc(idx_loaded[half], 16)

            def stack(c, n):
                ring, par = n % STACK_RING, n % 2
                wait_alone(sp, low_ready, c * GROUPS + (n + 1))
                m = n - 2
                if m >= 0 or not isinstance(c, int) or c > 0:
                    cc, mm = (c, m) if m >= 0 else (c - 1, m + GROUPS)
                    wait_alone(sp, stacked[mm % STACK_RING], cc * 256 + 128 * (mm // STACK_RING + 1))
                sp.dma_start(parts_dram[par].rearrange("k q e b -> (q e) k b"),
                             parts[:, par]).then_inc(parts_stored[par], 16)
                wait_alone(sp, parts_stored[par], c * 80 + 16 * (n // 2 + 1))
                if n >= STACK_RING:
                    wait_alone(sp, t_ready, c * UNITS + (n - STACK_RING + 1) ** 2)
                else:
                    wait_alone(sp, t_ready, (c - 1) * UNITS + (n + STACK_RING + 1) ** 2)
                for s, k in enumerate((0, 1, 0, 1)):
                    sp.dma_start(stack_main[DIM * s:DIM * (s + 1), ring],
                                 parts_dram[par, k].rearrange("q e b -> e q b")).then_inc(stacked[ring], 16)
                for half in range(2):
                    src = parts_dram[par].rearrange("k (v h) e b -> k h e v b", h=2)
                    for s, k in enumerate((2, 0)):
                        row = 64 * half + DIM * s
                        sp.dma_start(stack_fine[row:row + DIM, ring], src[k, half]).then_inc(stacked[ring], 16)

            load_idx(0, 0)
            sp.dma_start(hot_row[:, :], hot_rows).then_inc(hot_loaded[0], 16)
            for m in range(HOT_STEPS):
                for i, (n, _, f, blocks) in enumerate(hot):
                    if n == m:
                        sp.dma_start(hot_idx[i],
                                     hot_ids[i:i + 1, :].broadcast_to([P, CHUNK])).then_inc(hot_loaded[m], 16)
                        sp.dma_start(hot_table[i][0:tables[f].shape[0] // blocks, 0:blocks * DIM],
                                     tables[f].rearrange("(p b) d -> p (b d)", b=blocks)).then_inc(hot_loaded[m], 16)
                if m == 0:
                    load_raw(0)
                    sp.dma_start(ident_sb[:, :], ident).then_inc(ident_loaded, 16)
            load_idx(0, 1)
            sp.dma_start(sel[:, :, :], select).then_inc(consts_loaded, 16)
            sp.dma_start(w2_sb[:, :, :], w2).then_inc(consts_loaded, 16)
            sp.dma_start(w3_sb[:, :], w3).then_inc(consts_loaded, 16)
            sp.dma_start(b1_sb[:, :], b1).then_inc(consts_loaded, 16)
            sp.dma_start(b2_sb[:, :], b2).then_inc(consts_loaded, 16)

            def body(c, order):
                for step, *a in order:
                    if step == "split" and a[0] + 1 < PIECES:
                        load_raw(a[0] + 1)
                    elif step == "lows":
                        spread_piece(a[0])
                    elif step == "unit" and a[0] == UNITS // 2 and is_first(c):
                        sp.wait_ge(hot_ready, HOTS)
                        sp.dma_start(w1_sb[:, :, :], w1).then_inc(w1_loaded, 16)
                    elif step == "zout" and a[1] == ZBLOCKS - 1:
                        wait_alone(sp, z_out, (c + a[0]) * ZBLOCKS + ZBLOCKS)
                        sp.dma_start(z[ZDENSE:ZDENSE + DENSE, ZBLOCKS - 1, :],
                                     dense_t[c + a[0]]).then_inc(dense_loaded, 16)
                    if step == "low":
                        dc, n = a
                        stack(c + dc, n)
                        if dc == 1 and n == 0:
                            load_idx(c + 1, 1)
                        if dc == 0 and n == GATHER_RING and ("turn", 1, 0) in order:
                            load_idx(c + 1, 0)
            chunks(sp, body)

        @block.gpsimd
        def _(pool):
            def gather(c, n):
                g, ring, half = GROUPS - 1 - n, n % GATHER_RING, n // GATHER_RING
                if n % GATHER_RING == 0:
                    wait_alone(pool, idx_loaded[half], c * 16 + 16)
                wait_alone(pool, turned, c * GROUPS + (n - GATHER_RING + 1))
                for t in range(BT):
                    for q in gathered_fields(c, n):
                        f = PER * g + q
                        col = f - (1 - half) * (FIELDS // 2)
                        nc.gpsimd.indirect_dma_start(
                            gathered[:, ring, t, DIM * q:DIM * (q + 1)], None, tables[f],
                            bass.IndirectOffsetOnAxis(ap=idx[:, half, t, col:col + 1], axis=0),
                        ).then_inc(gather_done[ring], 16)

            for n in range(GROUPS):
                gather(0, n)
            with pool.Fori(1, CHUNKS) as c:
                for n in range(GROUPS):
                    gather(c, n)

        @block.tensor
        def _(pe):
            def turn(c, n):
                ring = n % GATHER_RING
                wait(pe, high_ready, c * GROUPS + n)
                if is_first(c) and n < HOT_STEPS:
                    pe.wait_ge(hot_loaded[n], hot_loads(n))
                    for k, b, i in hots(n):
                        _, q, f, blocks = hot[i]
                        parts_used = tables[f].shape[0] // blocks
                        pe.wait_ge(hot_ready, k + 1)
                        nc.tensor.matmul(turn_ps[DIM * q:DIM * (q + 1), :],
                                         hot_table[i][0:parts_used, DIM * b:DIM * (b + 1)],
                                         one_hots[0:parts_used, k % HOT_RING, :],
                                         start=(b == 0), stop=(b == blocks - 1)).then_inc(hot_used, 1)
                    pe.wait_ge(ident_loaded, 16)
                    pe.wait_ge(gather_done[ring], gathers(c, n))
                    for q in gathered_fields(c, n):
                        rows = slice(DIM * q, DIM * (q + 1))
                        for t in range(BT):
                            last = nc.tensor.matmul(turn_ps[rows, P * t:P * (t + 1)], gathered[:, ring, t, rows],
                                                    ident_sb[:, :], start=True, stop=True)
                    last.then_inc(turned, 1)
                    return
                pe.wait_ge(gather_done[ring], gathers(c, n))
                for t in range(BT):
                    last = nc.tensor.transpose(turn_ps[:, P * t:P * (t + 1)],
                                               gathered[:, ring, t, :], ident_sb[:, :])
                last.then_inc(turned, 1)

            def main(out_ap, u, half, cols, ring, q):
                at = P * main_tile(u, half)
                nc.tensor.matmul(out_ap, w_main[:, at + cols.start:at + cols.stop],
                                 stack_main[:, ring, q, :], start=True, stop=False)

            def fine(out_ap, u, half, cols, ring, q):
                rows = slice(64 * half, 64 * half + 64)
                return nc.tensor.matmul(out_ap, w_fine[rows, P * u + cols.start:P * u + cols.stop],
                                        stack_fine[rows, ring, q // 2, :], start=False, stop=True)

            def unit(c, u, first):
                n, g, h, v = unit_of(u)
                ring, slot = n % STACK_RING, 2 * t_slot(u, first)
                if u == n * n:
                    pe.wait_ge(stacked[ring], c * 256 + 128 * (n // STACK_RING + 1))
                if first and u % PIECE_UNITS == 0:
                    pe.wait_ge(w_loaded[u // PIECE_UNITS], 128)
                if first or u < MLP_BEHIND or u >= MLP_BEHIND + T_RING:
                    wait(pe, p_ready, c * UNITS + (u - T_RING + 1))
                elif u == MLP_BEHIND + 1:
                    pe.wait_ge(y_copied, c)
                if h != g:
                    for half in range(2):
                        main(t_ps[:, slot + half, :], u, half, slice(0, P), ring, 2 * v + half)
                    for half in range(2):
                        last = fine(t_ps[:, slot + half, :], u, half, slice(0, P), ring, 2 * v + half)
                else:
                    for half, blocks in enumerate((X_TILE, Y_TILE)):
                        for p, q in blocks:
                            cols = slice(DIM * p, DIM * (p + 1))
                            main(t_ps[cols, slot + half, :], u, half, cols, ring, q)
                        for p, q in blocks:
                            cols = slice(DIM * p, DIM * (p + 1))
                            last = fine(t_ps[cols, slot + half, :], u, half, cols, ring, q)
                last.then_inc(t_ready, 1)

            def sum_pairs(c, b):
                if b == 0:
                    pe.wait_ge(consts_loaded, 16 * N_CONST)
                k, r = b // PER_BLOCK, b % PER_BLOCK
                pe.wait_ge(p_ready, c * UNITS + (2 * b + 2))
                if r == 0:
                    wait(pe, z_out, c * ZBLOCKS + k)
                for j in range(BATCH_TILES):
                    at = (BATCH_TILES * b + j) % (2 * PRODUCT_RING)
                    last = nc.tensor.matmul(z_ps[DIM * j:DIM * (j + 1), :], sel[:, r, :], prod[:, at, :],
                                            start=(r == 0), stop=(r == PER_BLOCK - 1 or b == REDUCTIONS - 1))
                last.then_inc(summed, 1)

            def layer1(c, units, banks):
                pe.wait_ge(w1_loaded, 16)
                for k in range(ZBLOCKS):
                    if k in (0, ZBLOCKS - 2, ZBLOCKS - 1):
                        pe.wait_ge(z_out, c * ZBLOCKS + max(k + 1, ZBLOCKS - 2))
                    if k == ZBLOCKS - 1:
                        pe.wait_ge(dense_loaded, c * 16 + 16)
                    for m in range(M1):
                        if k == 0 and m % 2 == 0:
                            pe.wait_ge(p_ready, units + (m // 2 - 2))
                        last = nc.tensor.matmul(t_ps[:, banks[m], :], w1_sb[:, k, P * m:P * (m + 1)],
                                                z[:, k, :], start=(k == 0), stop=(k == ZBLOCKS - 1))
                        if k == ZBLOCKS - 1:
                            last.then_inc(h1_ready, 1)

            def layers23(c, units, banks):
                pe.wait_ge(p_ready, units)
                for k in range(M1):
                    pe.wait_ge(a1_ready, c * M1 + (k + 1))
                    for m in range(M2):
                        last = nc.tensor.matmul(t_ps[:, banks[M1 + m], :], w2_sb[:, k, P * m:P * (m + 1)], h1[:, k, :],
                                                start=(k == 0), stop=(k == M1 - 1))
                        if k == M1 - 1:
                            last.then_inc(h2_ready, 1)
                for k in range(M2):
                    pe.wait_ge(a2_ready, c * M2 + (k + 1))
                    last = nc.tensor.matmul(t_ps[0:1, banks[0], :], w3_sb[:, k:k + 1], h2[:, k, :],
                                            start=(k == 0), stop=(k == M2 - 1))
                last.then_inc(y_ready, 1)

            def body(c, order):
                for step, *a in order:
                    if step == "turn":
                        turn(c + a[0], a[1])
                    elif step == "unit":
                        unit(c, a[0], is_first(c))
                    elif step == "sum":
                        sum_pairs(c + a[0], a[1])
                    elif step in ("layer1", "layers23"):
                        units = UNITS if a[0] == 0 else MLP_BEHIND
                        layers = layer1 if step == "layer1" else layers23
                        layers(c + a[0], c * UNITS + units, mlp_banks(units))
            chunks(pe, body)

        @block.scalar
        def _(act):
            def high(c, n):
                g = GROUPS - 1 - n
                act.wait_ge(turned, c * GROUPS + (n + 1))
                wait(act, p_ready, (c - 1) * UNITS + min(83 + 2 * n, UNITS))
                nc.scalar.copy(emb[:, g, :], turn_ps[:, :])
                wait(act, parts_stored[n % 2], c * 80 + 16 * (n // 2))
                nc.scalar.copy(parts[:, n % 2, 0, :], turn_ps[:, :]).then_inc(high_ready, 1)

            def middle(c, n):
                act.wait_ge(rest_ready, c * GROUPS + (n + 1))
                nc.scalar.copy(parts[:, n % 2, 1, :], rest[:, :]).then_inc(middle_ready, 1)

            def w_high_of(k):
                act.wait_ge(raw_loaded, 16 * (k + 1))
                if k > 0:
                    act.wait_ge(w_loaded[k - 1], 128)
                nc.scalar.copy(w_parts[:, 0, :], w_raw).then_inc(w_high, 1)

            def w_middle_of(k):
                act.wait_ge(w_rest_ready, k + 1)
                nc.scalar.copy(w_parts[:, 1, :], w_rest).then_inc(w_middle, 1)

            def zout(c, k):
                act.wait_ge(summed, c * REDUCTIONS + min(PER_BLOCK * (k + 1), REDUCTIONS))
                if k == 0:
                    wait(act, h1_ready, c * M1)
                nc.scalar.copy(z[:, k, :], z_ps[:, :]).then_inc(z_out, 1)

            def layer1(c, banks):
                act.wait_ge(consts_loaded, 16 * N_CONST)
                for m in range(M1):
                    act.wait_ge(h1_ready, c * M1 + (m + 1))
                    if m == 0:
                        wait(act, y_stored, c * 16)
                    nc.scalar.activation(h1[:, m, :], t_ps[:, banks[m], :], ACT.Relu,
                                         bias=b1_sb[:, m:m + 1]).then_inc(a1_ready, 1)

            def layers23(c, banks):
                for m in range(M2):
                    act.wait_ge(h2_ready, c * M2 + (m + 1))
                    nc.scalar.activation(h2[:, m, :], t_ps[:, banks[M1 + m], :], ACT.Relu,
                                         bias=b2_sb[:, m:m + 1]).then_inc(a2_ready, 1)
                act.wait_ge(y_ready, c + 1)
                nc.scalar.copy(h1[0:1, 0, :], t_ps[0:1, banks[0], :]).then_inc(y_copied, 1)
                act.wait_ge(y_copied, c + 1)
                act.dma_start(out[c], h1[0:1, 0, :]).then_inc(y_stored, 16)

            def body(c, order):
                for step, *a in order:
                    if step == "turn":
                        high(c + a[0], a[1])
                    elif step == "rest":
                        middle(c + a[0], a[1])
                    elif step == "split":
                        w_high_of(a[0])
                    elif step == "lows":
                        w_middle_of(a[0])
                    elif step == "zout":
                        zout(c + a[0], a[1])
                    elif step in ("layer1", "layers23"):
                        layers = layer1 if step == "layer1" else layers23
                        layers(c + a[0], mlp_banks(UNITS if a[0] == 0 else MLP_BEHIND))
            chunks(act, body)
            act.wait_ge(y_stored, 16 * CHUNKS)

        @block.vector
        def _(dve):
            def one_hot_of(n, part):
                dve.wait_ge(hot_loaded[n], hot_loads(n))
                for k, b, i in (hots(n)[HOT_RING:] if part else hots(n)[:HOT_RING]):
                    parts_used = tables[hot[i][2]].shape[0] // hot[i][3]
                    wait(dve, hot_used, k - HOT_RING + 1)
                    nc.vector.tensor_scalar(one_hots[0:parts_used, k % HOT_RING, :],
                                            hot_idx[i][0:parts_used, :],
                                            hot_row[0:parts_used, HOT_BLOCKS * i + b:HOT_BLOCKS * i + b + 1], None,
                                            ALU.is_equal).then_inc(hot_ready, 1)

            def rest_of(c, n):
                g = GROUPS - 1 - n
                dve.wait_ge(high_ready, c * GROUPS + (n + 1))
                wait(dve, low_ready, c * GROUPS + n)
                nc.vector.tensor_tensor(rest[:, :], emb[:, g, :], parts[:, n % 2, 0, :],
                                        ALU.subtract).then_inc(rest_ready, 1)

            def low_of(c, n):
                dve.wait_ge(middle_ready, c * GROUPS + (n + 1))
                nc.vector.tensor_tensor(parts[:, n % 2, 2, :], rest[:, :], parts[:, n % 2, 1, :],
                                        ALU.subtract).then_inc(low_ready, 1)

            def w_rest_of(k):
                dve.wait_ge(w_high, k + 1)
                wait(dve, w_low, k)
                nc.vector.tensor_tensor(w_rest, w_raw, w_parts[:, 0, :], ALU.subtract).then_inc(w_rest_ready, 1)

            def w_low_of(k):
                dve.wait_ge(w_middle, k + 1)
                nc.vector.tensor_tensor(w_parts[:, 2, :], w_rest, w_parts[:, 1, :],
                                        ALU.subtract).then_inc(w_low, 1)

            def unit(c, u):
                _, _, h, _ = unit_of(u)
                dve.wait_ge(t_ready, c * UNITS + (u + 1))
                if u % 2 == 0:
                    wait(dve, summed, c * REDUCTIONS + (u // 2 - 1))
                slot, at = 2 * t_slot(u, is_first(c)), 2 * (u % PRODUCT_RING)
                second = emb[:, h:h + 1, :].broadcast_to([P, 2, CHUNK])
                nc.vector.tensor_tensor(prod[:, at:at + 2, :], t_ps[:, slot:slot + 2, :], second,
                                        ALU.mult).then_inc(p_ready, 1)

            def body(c, order):
                for step, *a in order:
                    if step == "rest":
                        rest_of(c + a[0], a[1])
                    elif step == "low":
                        low_of(c + a[0], a[1])
                    elif step == "hot":
                        one_hot_of(*a)
                    elif step == "split":
                        w_rest_of(a[0])
                    elif step == "lows":
                        w_low_of(a[0])
                    elif step == "unit":
                        unit(c, a[0])
            chunks(dve, body)


def pair_number(i, j):
    return i * FIELDS - i * (i + 1) // 2 + (j - i - 1)


def tile_pairs():
    tiles = []
    for u in range(UNITS):
        _, g, h, v = unit_of(u)
        f, s = PER * g, PER * h
        if h != g:
            for half in range(2):
                i = f + 2 * v + half
                tiles.append([(pair_number(i, s + p), False) for p in range(PER)])
        else:
            tiles.append([None, (pair_number(f, f + 1), False), (pair_number(f, f + 2), False),
                          (pair_number(f + 2, f + 3), False)])
            tiles.append([(pair_number(f, f + 3), True), None, (pair_number(f + 1, f + 2), False),
                          (pair_number(f + 1, f + 3), False)])
    return tiles


def z_row(t, p):
    block, t = divmod(t, BATCH_TILES * PER_BLOCK)
    return block, DIM * (t % BATCH_TILES) + PER * (t // BATCH_TILES) + p


def kernel(**inputs):
    import numpy as np
    import concourse.bacc as bacc
    from concourse.bass_utils import run_bass_kernel_spmd

    a = {k: np.asarray(v) for k, v in inputs.items()}
    pairs = a["L0_rec_W"]
    turned = pairs.transpose(0, 2, 1)
    w_pairs = np.zeros((PIECES, DIM, TILES // PIECES, PER, DIM), np.float32)
    w1 = np.zeros((P, ZBLOCKS, H1), np.float32)
    for t, blocks in enumerate(tile_pairs()):
        piece, at = divmod(main_tile(t // 2, t % 2), TILES // PIECES)
        for p, what in enumerate(blocks):
            if what is None:
                continue
            k, is_turned = what
            w_pairs[piece, :, at, p, :] = turned[k] if is_turned else pairs[k]
            block, row = z_row(t, p)
            w1[row, block] = a["W_top1"][k]
    w1[ZDENSE:ZDENSE + DENSE, ZBLOCKS - 1] = a["W_top1"][-DENSE:]
    select = np.zeros((P, PER_BLOCK, DIM), np.float32)
    for r in range(PER_BLOCK):
        for p in range(PER):
            select[DIM * p:DIM * (p + 1), r, PER * r + p] = 1.0

    hot = one_hot([a[f"tbl_{f}"].shape[0] for f in range(FIELDS)])
    hot_ids = np.ascontiguousarray(a["ids"][0:CHUNK, [f for _, _, f, _ in hot]].T)
    hot_rows = np.zeros((P, len(hot), HOT_BLOCKS), np.float32)
    for i, (_, _, _, blocks) in enumerate(hot):
        hot_rows[:, i] = blocks * np.arange(P)[:, None] + np.arange(HOT_BLOCKS)
    hot_rows = hot_rows.reshape(P, -1)

    arrays = {
        "dense_t": np.ascontiguousarray(a["dense_ctx"].reshape(CHUNKS, CHUNK, DENSE).transpose(0, 2, 1)),
        "ids": np.ascontiguousarray(a["ids"].reshape(CHUNKS, BT, P, FIELDS).transpose(0, 2, 1, 3)),
        "hot_ids": hot_ids,
        "hot_rows": hot_rows,
        "w_pairs": w_pairs.reshape(PIECES, P, WCOLS),
        "w1": w1,
        "b1": np.ascontiguousarray(a["b_top1"].reshape(M1, P).T),
        "w2": np.ascontiguousarray(a["W_top2"].reshape(M1, P, H2).transpose(1, 0, 2)),
        "b2": np.ascontiguousarray(a["b_top2"].reshape(M2, P).T),
        "w3": np.ascontiguousarray(a["W_top3"].reshape(M2, P).T),
        "select": select,
        "ident": np.eye(P, dtype=np.float32),
    }
    for f in range(FIELDS):
        arrays[f"tbl_{f}"] = np.ascontiguousarray(a[f"tbl_{f}"])

    nc = bacc.Bacc("TRN2", target_bir_lowering=False, num_devices=1)
    aps = {k: nc.dram_tensor(k, v.shape, mybir.dt.from_np(v.dtype), kind="ExternalInput").ap()
           for k, v in arrays.items()}
    out = nc.dram_tensor("y", (CHUNKS, 1, CHUNK), F32, kind="ExternalOutput").ap()
    tower(nc, aps["dense_t"], aps["ids"], aps["hot_ids"], aps["hot_rows"],
          [aps[f"tbl_{f}"] for f in range(FIELDS)], aps["w_pairs"], aps["w1"],
          aps["b1"], aps["w2"], aps["b2"], aps["w3"], aps["select"], aps["ident"], out)
    r = run_bass_kernel_spmd(nc, [arrays], core_ids=[0])
    return r.results[0]["y"].reshape(BATCH, 1)
```
